# Optimizing a Trainium2 kernel written in Bass

```python
import numpy as np
import jax
import jax.numpy as jnp

def _softmax(x, axis=-1):
    return jax.nn.softmax(x, axis=axis)

def _gelu(x):
    return jax.nn.gelu(x, approximate=True)

def _silu(x):
    return jax.nn.silu(x)

def _sigmoid(x):
    return jax.nn.sigmoid(x)

def _layernorm(x, axis=-1, eps=1e-05):
    m = jnp.mean(x, axis=axis, keepdims=True)
    v = jnp.var(x, axis=axis, keepdims=True)
    return (x - m) / jnp.sqrt(v + eps)

def _scatter_add(tgt, idx, src, axis=0):
    return tgt.at[idx].add(src)

def _segment_sum(src, seg, n):
    return jax.ops.segment_sum(src, seg, n)
kernel_name = 'mk_dlrm_tower_d1_rec_r8_6db859'

def setup_inputs(seed: int=0):
    np.random.seed(seed)
    _w = jnp.asarray

    def _rec_inputs():
        import jax
        import jax.numpy as jnp
        _tk = jax.random.key(seed)
        dense_ctx = jax.random.normal(jax.random.fold_in(_tk, 190), (1024, 16), jnp.float32)
        ids = jnp.stack([jax.random.randint(jax.random.fold_in(_tk, 200 + f), (1024,), 0, v, jnp.int32) for f, v in enumerate([125000, 1000, 1000, 1000, 12500, 12500, 1250, 1250, 1250, 125000, 125000, 12500, 1250, 12500, 12500, 1250, 1250, 1000, 1250, 125000, 1000, 12500, 1250, 125000])], axis=1)
        tbl_0 = 0.05 * jax.random.normal(jax.random.fold_in(_tk, 500 + 0), (125000, 16), jnp.float32)
        tbl_1 = 0.05 * jax.random.normal(jax.random.fold_in(_tk, 500 + 1), (1000, 16), jnp.float32)
        tbl_2 = 0.05 * jax.random.normal(jax.random.fold_in(_tk, 500 + 2), (1000, 16), jnp.float32)
        tbl_3 = 0.05 * jax.random.normal(jax.random.fold_in(_tk, 500 + 3), (1000, 16), jnp.float32)
        tbl_4 = 0.05 * jax.random.normal(jax.random.fold_in(_tk, 500 + 4), (12500, 16), jnp.float32)
        tbl_5 = 0.05 * jax.random.normal(jax.random.fold_in(_tk, 500 + 5), (12500, 16), jnp.float32)
        tbl_6 = 0.05 * jax.random.normal(jax.random.fold_in(_tk, 500 + 6), (1250, 16), jnp.float32)
        tbl_7 = 0.05 * jax.random.normal(jax.random.fold_in(_tk, 500 + 7), (1250, 16), jnp.float32)
        tbl_8 = 0.05 * jax.random.normal(jax.random.fold_in(_tk, 500 + 8), (1250, 16), jnp.float32)
        tbl_9 = 0.05 * jax.random.normal(jax.random.fold_in(_tk, 500 + 9), (125000, 16), jnp.float32)
        tbl_10 = 0.05 * jax.random.normal(jax.random.fold_in(_tk, 500 + 10), (125000, 16), jnp.float32)
        tbl_11 = 0.05 * jax.random.normal(jax.random.fold_in(_tk, 500 + 11), (12500, 16), jnp.float32)
        tbl_12 = 0.05 * jax.random.normal(jax.random.fold_in(_tk, 500 + 12), (1250, 16), jnp.float32)
        tbl_13 = 0.05 * jax.random.normal(jax.random.fold_in(_tk, 500 + 13), (12500, 16), jnp.float32)
        tbl_14 = 0.05 * jax.random.normal(jax.random.fold_in(_tk, 500 + 14), (12500, 16), jnp.float32)
        tbl_15 = 0.05 * jax.random.normal(jax.random.fold_in(_tk, 500 + 15), (1250, 16), jnp.float32)
        tbl_16 = 0.05 * jax.random.normal(jax.random.fold_in(_tk, 500 + 16), (1250, 16), jnp.float32)
        tbl_17 = 0.05 * jax.random.normal(jax.random.fold_in(_tk, 500 + 17), (1000, 16), jnp.float32)
        tbl_18 = 0.05 * jax.random.normal(jax.random.fold_in(_tk, 500 + 18), (1250, 16), jnp.float32)
        tbl_19 = 0.05 * jax.random.normal(jax.random.fold_in(_tk, 500 + 19), (125000, 16), jnp.float32)
        tbl_20 = 0.05 * jax.random.normal(jax.random.fold_in(_tk, 500 + 20), (1000, 16), jnp.float32)
        tbl_21 = 0.05 * jax.random.normal(jax.random.fold_in(_tk, 500 + 21), (12500, 16), jnp.float32)
        tbl_22 = 0.05 * jax.random.normal(jax.random.fold_in(_tk, 500 + 22), (1250, 16), jnp.float32)
        tbl_23 = 0.05 * jax.random.normal(jax.random.fold_in(_tk, 500 + 23), (125000, 16), jnp.float32)
        _rk = jax.random.fold_in(_tk, 7)
        W_top1 = 0.0693375 * jax.random.normal(jax.random.fold_in(_tk, 801), (208, 512), jnp.float32)
        W_top2 = 0.0441942 * jax.random.normal(jax.random.fold_in(_tk, 802), (512, 256), jnp.float32)
        W_top3 = 0.0625 * jax.random.normal(jax.random.fold_in(_tk, 803), (256, 1), jnp.float32)
        b_top1 = jnp.zeros((512,), jnp.float32)
        b_top2 = jnp.zeros((256,), jnp.float32)
        return (dense_ctx, ids, tbl_0, tbl_1, tbl_2, tbl_3, tbl_4, tbl_5, tbl_6, tbl_7, tbl_8, tbl_9, tbl_10, tbl_11, tbl_12, tbl_13, tbl_14, tbl_15, tbl_16, tbl_17, tbl_18, tbl_19, tbl_20, tbl_21, tbl_22, tbl_23, W_top1, b_top1, W_top2, b_top2, W_top3)
    dense_ctx, ids, tbl_0, tbl_1, tbl_2, tbl_3, tbl_4, tbl_5, tbl_6, tbl_7, tbl_8, tbl_9, tbl_10, tbl_11, tbl_12, tbl_13, tbl_14, tbl_15, tbl_16, tbl_17, tbl_18, tbl_19, tbl_20, tbl_21, tbl_22, tbl_23, W_top1, b_top1, W_top2, b_top2, W_top3 = _rec_inputs()

    def _L0_rec_setup():
        import jax, jax.numpy as jnp
        import numpy as np
        B, F, D = (512, 24, 16)
        LAYER_SIZES = [64, 64, 64]

        def _cin_forward(X0, Ws):
            F_ = X0.shape[1]
            Xk = X0
            outs = []
            for W in Ws:
                H_prev = Xk.shape[1]
                Wr = W.reshape(F_, H_prev, W.shape[1])
                Xk = jnp.einsum('bfd,bhd,fho->bod', X0, Xk, Wr)
                outs.append(Xk.sum(axis=2))
            return jnp.concatenate(outs, axis=1)
        key = jax.random.key(seed)
        k0, k1, k2, k3 = jax.random.split(key, 4)
        X0 = jax.random.normal(k0, (B, F, D), dtype=jnp.float32)
        prev = F
        Ws = []
        for k, h in zip((k1, k2, k3), LAYER_SIZES):
            Ws.append(jax.random.normal(k, (prev * F, h), dtype=jnp.float32) * 0.01)
            prev = h
        return {'X0': X0, 'W0': Ws[0], 'W1': Ws[1], 'W2': Ws[2]}
    _L0_rec_all = _L0_rec_setup()
    _L0_rec_in = {k: v for k, v in _L0_rec_all.items() if k in ('W0', 'W1', 'W2')}
    del _L0_rec_all
    return {'dense_ctx': dense_ctx, 'ids': ids, 'tbl_0': tbl_0, 'tbl_1': tbl_1, 'tbl_2': tbl_2, 'tbl_3': tbl_3, 'tbl_4': tbl_4, 'tbl_5': tbl_5, 'tbl_6': tbl_6, 'tbl_7': tbl_7, 'tbl_8': tbl_8, 'tbl_9': tbl_9, 'tbl_10': tbl_10, 'tbl_11': tbl_11, 'tbl_12': tbl_12, 'tbl_13': tbl_13, 'tbl_14': tbl_14, 'tbl_15': tbl_15, 'tbl_16': tbl_16, 'tbl_17': tbl_17, 'tbl_18': tbl_18, 'tbl_19': tbl_19, 'tbl_20': tbl_20, 'tbl_21': tbl_21, 'tbl_22': tbl_22, 'tbl_23': tbl_23, 'W_top1': W_top1, 'b_top1': b_top1, 'W_top2': W_top2, 'b_top2': b_top2, 'W_top3': W_top3, 'L0_rec_W0': _L0_rec_in['W0'], 'L0_rec_W1': _L0_rec_in['W1'], 'L0_rec_W2': _L0_rec_in['W2']}

def reference(dense_ctx, ids, tbl_0, tbl_1, tbl_2, tbl_3, tbl_4, tbl_5, tbl_6, tbl_7, tbl_8, tbl_9, tbl_10, tbl_11, tbl_12, tbl_13, tbl_14, tbl_15, tbl_16, tbl_17, tbl_18, tbl_19, tbl_20, tbl_21, tbl_22, tbl_23, W_top1, b_top1, W_top2, b_top2, W_top3, L0_rec_W0, L0_rec_W1, L0_rec_W2):
    import jax
    import jax.numpy as jnp

    def _L0_rec_ref(X0, W0, W1, W2):
        import jax, jax.numpy as jnp
        import numpy as np
        B, F, D = (512, 24, 16)
        LAYER_SIZES = [64, 64, 64]

        def _cin_forward(X0, Ws):
            F_ = X0.shape[1]
            Xk = X0
            outs = []
            for W in Ws:
                H_prev = Xk.shape[1]
                Wr = W.reshape(F_, H_prev, W.shape[1])
                Xk = jnp.einsum('bfd,bhd,fho->bod', X0, Xk, Wr)
                outs.append(Xk.sum(axis=2))
            return jnp.concatenate(outs, axis=1)
        return _cin_forward(X0, (W0, W1, W2))
    e = jnp.stack([tbl_0[ids[:, 0]], tbl_1[ids[:, 1]], tbl_2[ids[:, 2]], tbl_3[ids[:, 3]], tbl_4[ids[:, 4]], tbl_5[ids[:, 5]], tbl_6[ids[:, 6]], tbl_7[ids[:, 7]], tbl_8[ids[:, 8]], tbl_9[ids[:, 9]], tbl_10[ids[:, 10]], tbl_11[ids[:, 11]], tbl_12[ids[:, 12]], tbl_13[ids[:, 13]], tbl_14[ids[:, 14]], tbl_15[ids[:, 15]], tbl_16[ids[:, 16]], tbl_17[ids[:, 17]], tbl_18[ids[:, 18]], tbl_19[ids[:, 19]], tbl_20[ids[:, 20]], tbl_21[ids[:, 21]], tbl_22[ids[:, 22]], tbl_23[ids[:, 23]]], axis=1)
    z = _L0_rec_ref(e, L0_rec_W0, L0_rec_W1, L0_rec_W2)
    z = z.reshape(z.shape[0], -1)
    h = jnp.concatenate([z, dense_ctx], axis=1)
    h = jnp.maximum(h @ W_top1 + b_top1, 0.0)
    h = jnp.maximum(h @ W_top2 + b_top2, 0.0)
    y = h @ W_top3
    return y

_drawn_inputs = setup_inputs


def setup_inputs(seed=0):
    import zlib

    import numpy as np

    out = dict(_drawn_inputs(seed))
    spreads = {'b_top1': (0.0, 0.1), 'b_top2': (0.0, 0.1)}
    factors = {'tbl_0': 8.0,
     'tbl_1': 8.0,
     'tbl_2': 8.0,
     'tbl_3': 8.0,
     'tbl_4': 8.0,
     'tbl_5': 8.0,
     'tbl_6': 8.0,
     'tbl_7': 8.0,
     'tbl_8': 8.0,
     'tbl_9': 8.0,
     'tbl_10': 8.0,
     'tbl_11': 8.0,
     'tbl_12': 8.0,
     'tbl_13': 8.0,
     'tbl_14': 8.0,
     'tbl_15': 8.0,
     'tbl_16': 8.0,
     'tbl_17': 8.0,
     'tbl_18': 8.0,
     'tbl_19': 8.0,
     'tbl_20': 8.0,
     'tbl_21': 8.0,
     'tbl_22': 8.0,
     'tbl_23': 8.0,
     'L0_rec_W0': 8.0,
     'L0_rec_W1': 8.0,
     'L0_rec_W2': 8.0}
    for name, (base, spread) in spreads.items():
        noise = np.random.default_rng([zlib.crc32(name.encode()), seed]).standard_normal(out[name].shape)
        drawn = base * np.exp(spread * noise) if base else spread * noise
        out[name] = jnp.asarray(drawn.astype(out[name].dtype))
    for name, factor in factors.items():
        out[name] = (out[name] * factor).astype(out[name].dtype)
    return out
```

```python
from contextlib import ExitStack

import concourse.bass as bass
from concourse import mybir

ALU = mybir.AluOpType
ACT = mybir.ActivationFunctionType
F32 = mybir.dt.float32
F32R = mybir.dt.float32r
I32 = mybir.dt.int32
AX_X = mybir.AxisListType.X

B, F, D, H = 1024, 24, 16, 64
N_TABLES = F
DENSE = 16
TOP1, TOP2 = 512, 256

P = 128
NBLK = B // P
HS = P // 2
NU = 2 * NBLK
DH = D // 2
NT = DH * HS
FP = 2
NC = F // FP
GRP = 8
NG = HS // GRP
GC = F + 1

SHIFTS = [[1, 2, 3, 4, 5], [6, 7, 8, 9, 10], [11, 0, 12]]
ROWS0 = [F * len(s) for s in SHIFTS]
BOTH = [ROWS0[0], ROWS0[1], F]
R0 = ROWS0[0]

SEL1 = 0
SEL0 = SEL1 + NC * P
SELT = SEL0 + 4 * R0
FOLD = SELT + 2 * F
N_SEL = FOLD + HS
IDENT = N_SEL
MASK = IDENT + P
N_CONST = MASK + GRP

ORDER = ["c0", "c1", "c2", "c3", "c4", "a", "c5", "b0", "c6", "b1", "c7", "b2", "c8", "c9", "c10", "c11"]
A_PLACE = ORDER.index("a")
NUMBER = {w: n for n, w in enumerate(w for w in ORDER if w != "a")}
LAST = [w for w in ORDER if w[0] == "c"]
HEAD = ["a", "b0", "b1", "b2"]
NZ = 3


def cin_tower(nc, t, out):
    with ExitStack() as ctx:
        def sb(name, shape, dt=F32):
            return ctx.enter_context(nc.sbuf_tensor(name, shape, dt))

        def sem(name):
            return ctx.enter_context(nc.semaphore(name))

        ids_sb = sb("ids_sb", [P, NBLK * F], I32)
        idx = sb("idx", [P, F], I32)
        emb = sb("emb", [P, F, D])
        consts = sb("consts", [P, N_CONST])
        sel = sb("sel", [P, N_SEL], F32R)
        parts = sb("parts", [P, D, P], F32R)
        xp = sb("xp", [P, HS, D], F32R)
        a0 = sb("a0", [P, 2, NT])
        x1 = sb("x1", [P, 2, 2, NT])
        prod = sb("prod", [P, NZ, 2, NT])
        x2 = sb("x2", [P, HS, D])
        x2t = sb("x2t", [P, NG, P])
        bd = sb("bd", [P, NG, 2, GRP, GC])
        gram = sb("gram", [P, GC, HS])
        z1h = sb("z1h", [P, 2, HS])
        z = sb("z", [P, 3, NBLK * HS])
        w0 = sb("w0", [P, 3, H])
        w0t = sb("w0t", [P, 3, H])
        w1 = sb("w1", [P, NC, H])
        w2 = sb("w2", [P, F, H])
        wt1 = sb("wt1", [P, 3, TOP1])
        wd = sb("wd", [P, TOP1])
        wt2 = sb("wt2", [P, TOP1 // P, TOP2])
        wt3 = sb("wt3", [P, TOP2 // P])
        bt1 = sb("bt1", [P, TOP1 // P])
        bt2 = sb("bt2", [P, TOP2 // P])
        dense = sb("dense", [P, NBLK, DENSE])
        dt = sb("dt", [P, NBLK, HS])
        h1 = sb("h1", [P, TOP1 // P, 2, NBLK * HS])
        h2 = sb("h2", [P, TOP2 // P, 2, NBLK * HS])
        y = sb("y", [1, P, NBLK])

        ps = ctx.enter_context(nc.psum_tensor("ps", [P, 8, 512], F32))
        X1B, X2B, M0, M1 = 4, 5, 6, 7

        ids_loaded = sem("ids_loaded")
        consts_loaded = sem("consts_loaded")
        cin_loaded = sem("cin_loaded")
        dense_loaded = sem("dense_loaded")
        top_loaded = sem("top_loaded")
        idx_ready = sem("idx_ready")
        gathered = sem("gathered")
        zeroed = sem("zeroed")
        sel_ready = sem("sel_ready")
        w0_ready = sem("w0_ready")
        bd_ones = sem("bd_ones")
        hi_split = sem("hi_split")
        lo_split = sem("lo_split")
        xp_ready = sem("xp_ready")
        xp_copied = sem("xp_copied")
        filled = sem("filled")
        a0_copied = sem("a0_copied")
        multiplied = sem("multiplied")
        summed = sem("summed")
        x1_copied = sem("x1_copied")
        z1_reduced = sem("z1_reduced")
        z1_added = sem("z1_added")
        x2_copied = sem("x2_copied")
        x0t_ready = sem("x0t_ready")
        bd_built = sem("bd_built")
        x2t_ready = sem("x2t_ready")
        x2t_copied = sem("x2t_copied")
        gram_ready = sem("gram_ready")
        gram_copied = sem("gram_copied")
        z2_copied = sem("z2_copied")
        z3_ready = sem("z3_ready")
        z3_copied = sem("z3_copied")
        dense_turned = sem("dense_turned")
        dense_copied = sem("dense_copied")
        h1_ready = sem("h1_ready")
        h1_copied = sem("h1_copied")
        h2_ready = sem("h2_ready")
        h2_copied = sem("h2_copied")
        y_ready = sem("y_ready")
        y_copied = sem("y_copied")
        stored = sem("stored")

        ident = consts[:, IDENT:IDENT + P]
        mask = consts[:, MASK:MASK + GRP]

        def fills_before(u):
            return 4 + 16 * u

        def products_before(u):
            return 3 + 15 * u

        def slot(q):
            return 2 * (q % 2)

        block = ctx.enter_context(nc.Block())

        @block.sync
        def _(sp):
            sp.dma_start(ids_sb[:, :], t["ids"].rearrange("(s k) f -> s (k f)", k=NBLK)).then_inc(ids_loaded, 16)
            sp.dma_start(consts[:, :], t["consts"]).then_inc(consts_loaded, 16)
            for j, w in ((0, w0), (1, w0t)):
                sp.dma_start(w[0:R0, 0:2, :], t["W0_pairs"][j, 0:2 * R0, :].rearrange("(c r) o -> r c o", c=2)
                             ).then_inc(cin_loaded, 16)
                sp.dma_start(w[0:ROWS0[2], 2, :], t["W0_pairs"][j, 2 * R0:2 * R0 + ROWS0[2], :]
                             ).then_inc(cin_loaded, 16)
            sp.dma_start(w1[:, :, :], t["L0_rec_W1"].rearrange("(c r) o -> r c o", r=P)).then_inc(cin_loaded, 16)
            for p in range(2):
                sp.dma_start(w2[HS * p:HS * p + H, :, :], t["L0_rec_W2"].rearrange("(f h) o -> h f o", h=H)
                             ).then_inc(cin_loaded, 16)
            sp.dma_start(dense[:, :, :], t["dense_ctx"].rearrange("(s k) c -> s k c", k=NBLK)).then_inc(dense_loaded, 16)
            sp.wait_ge(zeroed, 3)
            for p in range(2):
                rows = slice(HS * p, HS * p + H)
                sp.dma_start(wt1[rows, :, :], t["W_top1"][0:3 * H, :].rearrange("(z r) m -> r z m", r=H)
                             ).then_inc(top_loaded, 16)
                sp.dma_start(wd[HS * p:HS * p + DENSE, :], t["W_top1"][3 * H:3 * H + DENSE, :]).then_inc(top_loaded, 16)
            sp.dma_start(wt2[:, :, :], t["W_top2"].rearrange("(r c) m -> r c m", r=P)).then_inc(top_loaded, 16)
            sp.dma_start(wt3[:, :], t["W_top3"].rearrange("(r c) m -> r (c m)", r=P)).then_inc(top_loaded, 16)
            sp.dma_start(bt1[:, :], t["b_top1"].rearrange("(r c) -> r c", r=P)).then_inc(top_loaded, 16)
            sp.dma_start(bt2[:, :], t["b_top2"].rearrange("(r c) -> r c", r=P)).then_inc(top_loaded, 16)
            sp.wait_ge(y_copied, 2)
            sp.dma_start(out.rearrange("(a s) k -> a (s k)", a=1), y[:, :, :].rearrange("a s k -> a (s k)")
                         ).then_inc(stored, 16)
            sp.wait_ge(stored, 16)

        N_CIN, N_TOP = 7 * 16, 8 * 16

        @block.gpsimd
        def _(pool):
            pool.memset(wd[:, :], 0.0).then_inc(zeroed, 1)
            pool.memset(dt[:, :, :], 0.0).then_inc(zeroed, 1)
            def gather():
                for f in range(F):
                    pool.indirect_dma_start(emb[:, f, :], None, t[f"tbl_{f}"],
                                            bass.IndirectOffsetOnAxis(ap=idx[:, f:f + 1], axis=0)
                                            ).then_inc(gathered, 16)

            pool.wait_ge(ids_loaded, 16)
            pool.tensor_copy(idx[:, :], ids_sb[:, 0:F]).then_inc(idx_ready, 1)
            pool.wait_ge(idx_ready, 1)
            with pool.Fori(0, NBLK - 1) as k:
                gather()
                pool.wait_ge(lo_split, k + 1)
                pool.tensor_copy(idx[:, :], ids_sb[:, bass.ds(k * F + F, F)]).then_inc(idx_ready, 1)
                pool.wait_ge(idx_ready, k + 2)
            gather()

        @block.scalar
        def _(act):
            def split_high(k):
                act.wait_ge(gathered, (k + 1) * (16 * F))
                act.wait_ge(xp_ready, 2 * k)
                for p in range(2):
                    rows = slice(HS * p, HS * p + HS)
                    ins = nc.scalar.activation(parts[rows, :, HS * p:HS * p + F],
                                               emb[rows, :, :].rearrange("s f d -> s d f"), ACT.Copy)
                ins.then_inc(hi_split, 1)

            def copy_xp(k, h):
                act.wait_ge(xp_ready, 2 * k + h + 1)
                nc.scalar.activation(xp[:, :, DH * h:DH * h + DH].rearrange("r s d -> r d s"),
                                     ps[:, M1, :].rearrange("r (d s) -> r d s", s=HS),
                                     ACT.Copy).then_inc(xp_copied, 1)

            def copy_a0(u, n, q):
                act.wait_ge(filled, n + 1)
                s = slot(q)
                nc.scalar.activation(a0[0:R0, :, :], ps[0:R0, s:s + 2, :], ACT.Copy).then_inc(a0_copied, 1)

            def copy_x1(u, par, head=False):
                act.wait_ge(summed, products_before(u - 1) + NUMBER["b2"] + 1 if not head else 3)
                for twice in range(2):
                    for p in range(2):
                        ins = nc.scalar.activation(x1[HS * twice:HS * twice + H, par, p, :],
                                                   ps[HS * p:HS * p + H, X1B, :], ACT.Copy)
                ins.then_inc(x1_copied, 1)

            def copy_x2(u, h, last=False):
                act.wait_ge(summed, products_before(u) + (NC if last else len(NUMBER)))
                nc.scalar.activation(x2[:, :, DH * h:DH * h + DH], ps[:, X2B, :].rearrange("r (s d) -> r s d", d=DH),
                                     ACT.Copy).then_inc(x2_copied, 1)

            def build_bd(k):
                act.wait_ge(x0t_ready, k + 1)
                for j in range(GRP):
                    ins = nc.scalar.activation(bd[:, :, :, j, 0:F].rearrange("r g p f -> r (g p) f"),
                                               ps[:, M0, 0:NG * 2 * F].rearrange("r (a f) -> r a f", f=F),
                                               ACT.Copy, scale=mask[:, j:j + 1])
                ins.then_inc(bd_built, 1)

            def copy_x2t(k, j):
                act.wait_ge(x2t_ready, 2 * k + j + 1)
                nc.scalar.activation(x2t[:, 4 * j:4 * j + 4, :].rearrange("r g c -> r (g c)"), ps[:, M0 + j, :],
                                     ACT.Copy).then_inc(x2t_copied, 1)

            def copy_gram(k, j):
                act.wait_ge(gram_ready, 4 * k + j + 1)
                if j == 0:
                    act.wait_ge(z2_copied, k)
                n = 2 * GRP
                nc.scalar.activation(gram[:, :, n * j:n * j + n].rearrange("r f s -> r s f"),
                                     ps[:, M0 + j % 2, 0:n * GC].rearrange("r (s f) -> r s f", f=GC),
                                     ACT.Copy).then_inc(gram_copied, 1)

            def copy_z3(k):
                act.wait_ge(z3_ready, k + 1)
                for p in range(2):
                    rows = slice(HS * p, HS * p + H)
                    ins = nc.scalar.activation(z[rows, 2, bass.ds(k * HS, HS)], ps[rows, M0 + p, 0:HS], ACT.Copy)
                ins.then_inc(z3_copied, 1)

            act.wait_ge(consts_loaded, 16)
            act.wait_ge(dense_turned, 1)
            act.wait_ge(zeroed, 3)
            for p in range(2):
                ins = nc.scalar.activation(
                    dt[HS * p:HS * p + DENSE, :, :],
                    ps[0:DENSE, X1B:X1B + 2, :].rearrange("c b (k s) -> c (b k) s", s=P)[:, :, HS * p:HS * p + HS],
                    ACT.Copy)
            ins.then_inc(dense_copied, 1)
            split_high(0)
            copy_xp(0, 0)
            copy_a0(0, 0, 0)
            copy_x1(0, 0, head=True)

            def odd_step(u, k, last=False):
                copy_x2(u - 1, 0)
                if not last:
                    split_high(k + 1)
                    copy_xp(k + 1, 0)
                    copy_a0(u + 1, fills_before(u) + A_PLACE, A_PLACE)
                build_bd(k)
                if not last:
                    copy_x1(u + 1, 0)

            def even_step(u, k, first=False):
                if not first:
                    copy_x2(u - 1, 1)
                copy_xp(k, 1)
                if not first:
                    copy_x2t(k - 1, 0)
                    copy_x2t(k - 1, 1)
                copy_a0(u + 1, fills_before(u) + A_PLACE, A_PLACE)
                if not first:
                    for j in range(4):
                        copy_gram(k - 1, j)
                copy_x1(u + 1, 1)
                if not first:
                    copy_z3(k - 1)

            even_step(0, 0, first=True)
            with act.Fori(0, NBLK - 1) as i:
                odd_step(2 * i + 1, i)
                even_step(2 * i + 2, i + 1)
            odd_step(NU - 1, NBLK - 1, last=True)
            copy_x2(NU - 1, 1, last=True)
            for j in range(2):
                copy_x2t(NBLK - 1, j)
            for j in range(4):
                copy_gram(NBLK - 1, j)
            copy_z3(NBLK - 1)

            act.wait_ge(top_loaded, N_TOP)
            for m in range(TOP1 // P):
                act.wait_ge(h1_ready, m + 1)
                for p in range(2):
                    ins = nc.scalar.activation(h1[:, m, p, :], ps[:, 2 * m + p, :], ACT.Relu, bias=bt1[:, m:m + 1])
                ins.then_inc(h1_copied, 1)
            for m in range(TOP2 // P):
                act.wait_ge(h2_ready, m + 1)
                for p in range(2):
                    ins = nc.scalar.activation(h2[:, m, p, :], ps[:, 2 * m + p, :], ACT.Relu, bias=bt2[:, m:m + 1])
                ins.then_inc(h2_copied, 1)
            for p in range(2):
                act.wait_ge(y_ready, p + 1)
                nc.scalar.activation(y[:, HS * p:HS * p + HS, :],
                                     ps[0:1, 4 + p, :].rearrange("a (k s) -> a s k", k=NBLK),
                                     ACT.Copy).then_inc(y_copied, 1)

        @block.vector
        def _(dve):
            def split_low(k):
                dve.wait_ge(hi_split, k + 1)
                for p in range(2):
                    rows = slice(HS * p, HS * p + HS)
                    c = HS * p
                    ins = nc.vector.tensor_tensor(parts[rows, :, c + F:c + 2 * F],
                                                  emb[rows, :, :].rearrange("s f d -> s d f"),
                                                  parts[rows, :, c:c + F], ALU.subtract)
                ins.then_inc(lo_split, 1)

            def multiply(what, par, nfill, nprod, q, n):
                dve.wait_ge(filled, nfill + 1)
                if n >= NZ:
                    dve.wait_ge(summed, nprod - NZ + 1)
                rows = P if what[0] == "c" else ROWS0[int(what[1])]
                other = x1[0:rows, par, :, :] if what[0] == "c" else a0[0:rows, :, :]
                nc.vector.tensor_tensor(prod[0:rows, n % NZ, :, :], ps[0:rows, slot(q):slot(q) + 2, :], other,
                                        ALU.mult).then_inc(multiplied, 1)

            def reduce_z1(u, h):
                dve.wait_ge(x1_copied, u + 1)
                nc.vector.tensor_reduce(z1h[:, h, :], ps[:, X1B, :].rearrange("r (s d) -> r s d", d=DH), AX_X, ALU.add
                                        ).then_inc(z1_reduced, 1)

            def add_z1(u, k):
                dve.wait_ge(z1_reduced, u + 1)
                nc.vector.tensor_tensor(z[:, 0, bass.ds(k * HS, HS)], z1h[:, 0, :], z1h[:, 1, :], ALU.add
                                        ).then_inc(z1_added, 1)

            def copy_z2(k):
                dve.wait_ge(gram_copied, 4 * k + 4)
                nc.vector.tensor_copy(z[:, 1, bass.ds(k * HS, HS)], gram[:, F, :]).then_inc(z2_copied, 1)

            def step(u, k, par, first=False, last=False):
                order = [w for w in (LAST if last else ORDER)]
                n = 0
                for q, what in enumerate(order):
                    if what == "a":
                        continue
                    if what == "c0":
                        dve.wait_ge(x1_copied, u + 1)
                    if what == "b0":
                        dve.wait_ge(a0_copied, u + 2)
                    multiply(what, par, fills_before(u) + q, products_before(u) + n, q, NZ + n)
                    n += 1
                    if q == 0:
                        reduce_z1(u, par)
                    if q == 2 and par == 1 and not last:
                        split_low(k + 1)
                    if q == 3 and par == 1:
                        add_z1(u, k)
                if par == 0 and not first:
                    copy_z2(k - 1)

            dve.memset(parts[:, :, :].bitcast(F32), 0.0).then_inc(zeroed, 1)
            dve.wait_ge(consts_loaded, 16)
            nc.vector.tensor_copy(sel[:, :], consts[:, 0:N_SEL]).then_inc(sel_ready, 1)
            nc.vector.tensor_copy(bd[:, :, :, :, F].rearrange("r g p j -> r (g p) j"),
                                  mask.unsqueeze(1).to_broadcast([P, 2 * NG, GRP])).then_inc(bd_ones, 1)
            dve.wait_ge(cin_loaded, N_CIN)
            for c in range(3):
                ins = nc.vector.tensor_tensor(w0[0:BOTH[c], c, :], w0[0:BOTH[c], c, :], w0t[0:BOTH[c], c, :], ALU.add)
            ins.then_inc(w0_ready, 1)
            split_low(0)
            dve.wait_ge(a0_copied, 1)
            for j in range(3):
                multiply(f"b{j}", 0, 1 + j, j, 1 + j, j)
            step(0, 0, 0, first=True)
            with dve.Fori(0, NBLK - 1) as i:
                step(2 * i + 1, i, 1)
                step(2 * i + 2, i + 1, 0)
            step(NU - 1, NBLK - 1, 1, last=True)
            copy_z2(NBLK - 1)

        @block.tensor
        def _(pe):
            def fill(what, q, h, free):
                s = slot(q)
                if free is not None:
                    pe.wait_ge(*free)
                if what[0] == "c":
                    col, m = SEL1 + int(what[1:]) * P, P
                else:
                    j = 0 if what == "a" else 1 + int(what[1])
                    col, m = SEL0 + j * R0, R0 if what == "a" else ROWS0[j - 1]
                for p in range(2):
                    rows = slice(HS * p, HS * p + 2 * F)
                    ins = nc.tensor.matmul(ps[0:m, s + p, :], sel[rows, col:col + m],
                                           xp[rows, :, DH * h:DH * h + DH],
                                           start=True, stop=True)
                ins.then_inc(filled, 1)

            def contract(what, nprod, n):
                pe.wait_ge(multiplied, nprod + 1)
                j = int(what[1:])
                if what[0] == "c":
                    rows, w, bank, end = P, w1[:, j, :], X2B, NC - 1
                else:
                    rows, w, bank, end = ROWS0[j], w0[0:ROWS0[j], j, :], X1B, 2
                for p in range(2):
                    ins = nc.tensor.matmul(ps[HS * p:HS * p + H, bank, :], w, prod[0:rows, n % NZ, p, :],
                                           start=j == 0, stop=j == end)
                ins.then_inc(summed, 1)

            def build_xp(k, h):
                for d in range(DH):
                    ins = nc.tensor.matmul(ps[:, M1, HS * d:HS * d + HS], parts[:, DH * h + d, :], sel[:, FOLD:FOLD + HS],
                                           start=True, stop=True)
                ins.then_inc(xp_ready, 1)

            def turn_x0(k):
                for g in range(NG):
                    ins = nc.tensor.matmul(ps[:, M0, 2 * F * g:2 * F * g + 2 * F], xp[:, GRP * g:GRP * g + GRP, :].rearrange("r s d -> r (s d)"),
                                           sel[:, SELT:SELT + 2 * F], start=True, stop=True)
                ins.then_inc(x0t_ready, 1)

            def turn_x2(k, j):
                for g in range(4):
                    gg = 4 * j + g
                    ins = nc.tensor.transpose(ps[:, M0 + j, P * g:P * g + P], x2[:, GRP * gg:GRP * gg + GRP, :].rearrange("r s d -> r (s d)"), ident)
                ins.then_inc(x2t_ready, 1)

            def grams(k, j):
                n = GRP * GC
                for g in range(2):
                    gg = 2 * j + g
                    for p in range(2):
                        ins = nc.tensor.matmul(ps[HS * p:HS * p + H, M0 + j % 2, n * g:n * g + n],
                                               x2t[:, gg, HS * p:HS * p + H],
                                               bd[:, gg, p, :, :].rearrange("r j f -> r (j f)"), start=True, stop=True)
                ins.then_inc(gram_ready, 1)

            def layer3(f0, f1):
                for f in range(f0, f1):
                    for p in range(2):
                        rows = slice(HS * p, HS * p + H)
                        ins = nc.tensor.matmul(ps[rows, M0 + p, 0:HS], w2[rows, f, :], gram[rows, f, :],
                                               start=f == 0, stop=f == F - 1)
                if f1 == F:
                    ins.then_inc(z3_ready, 1)

            def gram_extra(k, q, tail=False):
                if q == 3:
                    pe.wait_ge(x2_copied, 2 * k + 2)
                    pe.wait_ge(bd_built, k + 1)
                    turn_x2(k, 0)
                if q == 4:
                    if not tail:
                        pe.wait_ge(xp_copied, 2 * k + 4)
                    turn_x2(k, 1)
                if q == 6:
                    pe.wait_ge(x2t_copied, 2 * k + 1)
                    grams(k, 0)
                if q == 7:
                    pe.wait_ge(x2t_copied, 2 * k + 2)
                    grams(k, 1)
                if q == 9:
                    pe.wait_ge(gram_copied, 4 * k + 1)
                    grams(k, 2)
                if q == 11:
                    pe.wait_ge(gram_copied, 4 * k + 2)
                    grams(k, 3)
                if q == 13:
                    if tail:
                        pe.wait_ge(gram_copied, 4 * k + 4)
                    layer3(0, 8)
                if q == 14:
                    layer3(8, 16)
                if q == 15:
                    layer3(16, F)

            def extra(k, par, q, first, last):
                if par == 0:
                    if q == 1:
                        pe.wait_ge(xp_copied, 2 * k + 1)
                        build_xp(k, 1)
                    if not first:
                        gram_extra(k - 1, q)
                else:
                    if q == 1:
                        pe.wait_ge(z3_copied, k)
                        pe.wait_ge(xp_copied, 2 * k + 2)
                        turn_x0(k)
                    if q == 4 and not last:
                        pe.wait_ge(lo_split, k + 2)
                        build_xp(k + 1, 0)

            def step(u, k, par, first=False, last=False):
                order = LAST if last else ORDER
                filled_so_far = (HEAD if first else ORDER)[-2:] + order
                for q, what in enumerate(order):
                    old = filled_so_far[q]
                    if q < 2:
                        number = q - 2
                    elif old != "a":
                        number = NUMBER[old] if not last else q - 2
                    if what == "a":
                        pe.wait_ge(xp_copied, 2 * k + 2 + par)
                    if q == 13 and par == 0 and not first:
                        pe.wait_ge(gram_copied, 4 * k)
                    if old == "a":
                        fill(what, q, 1 - par if what[0] != "c" else par, (a0_copied, u + 2))
                    else:
                        fill(what, q, 1 - par if what[0] != "c" else par, (multiplied, products_before(u) + number + 1))
                        if old == "c0" and not first:
                            pe.wait_ge(x2_copied, u)
                        if old == "b0":
                            pe.wait_ge(z1_reduced, u + 1)
                        contract(old, products_before(u) + number, NZ + number)
                    extra(k, par, q, first, last)

            pe.wait_ge(consts_loaded, 16)
            pe.wait_ge(dense_loaded, 16)
            for k in range(NBLK):
                ins = nc.tensor.transpose(ps[0:DENSE, X1B + k // 4, P * (k % 4):P * (k % 4) + P], dense[:, k, :], ident)
            ins.then_inc(dense_turned, 1)
            pe.wait_ge(sel_ready, 1)
            pe.wait_ge(lo_split, 1)
            build_xp(0, 0)
            pe.wait_ge(xp_copied, 1)
            pe.wait_ge(w0_ready, 1)
            pe.wait_ge(cin_loaded, N_CIN)
            pe.wait_ge(bd_ones, 1)
            pe.wait_ge(dense_copied, 1)
            fill("a", 0, 0, None)
            fill("b0", 1, 0, None)
            fill("b1", 2, 0, (a0_copied, 1))
            fill("b2", 3, 0, (multiplied, 1))
            contract("b0", 0, 0)
            step(0, 0, 0, first=True)
            with pe.Fori(0, NBLK - 1) as i:
                step(2 * i + 1, i, 1)
                step(2 * i + 2, i + 1, 0)
            step(NU - 1, NBLK - 1, 1, last=True)
            done = products_before(NU - 1) + NC
            for n in (NC - 2, NC - 1):
                contract(f"c{n}", done - NC + n, NZ + n)
            for q in range(len(ORDER)):
                gram_extra(NBLK - 1, q, tail=True)

            pe.wait_ge(top_loaded, N_TOP)
            pe.wait_ge(z3_copied, NBLK)
            pe.wait_ge(z2_copied, NBLK)
            pe.wait_ge(z1_added, NBLK)
            for m in range(TOP1 // P):
                cols = slice(m, TOP1, TOP1 // P)
                for c in range(4):
                    for p in range(2):
                        rows = slice(HS * p, HS * p + HS)
                        w = wt1[rows, c, cols] if c < 3 else wd[rows, cols]
                        x = z[rows, c, :] if c < 3 else dt[rows, :, :].rearrange("r k s -> r (k s)")
                        ins = nc.tensor.matmul(ps[:, 2 * m + p, :], w, x, start=c == 0, stop=c == 3)
                ins.then_inc(h1_ready, 1)
            for m in range(TOP2 // P):
                for c in range(TOP1 // P):
                    pe.wait_ge(h1_copied, c + 1)
                    for p in range(2):
                        ins = nc.tensor.matmul(ps[:, 2 * m + p, :], wt2[:, c, m:TOP2:TOP2 // P], h1[:, c, p, :],
                                               start=c == 0, stop=c == TOP1 // P - 1)
                ins.then_inc(h2_ready, 1)
            for p in range(2):
                for c in range(TOP2 // P):
                    pe.wait_ge(h2_copied, c + 1)
                    ins = nc.tensor.matmul(ps[0:1, 4 + p, :], wt3[:, c:c + 1], h2[:, c, p, :],
                                           start=c == 0, stop=c == TOP2 // P - 1)
                ins.then_inc(y_ready, 1)


def selections():
    import numpy as np

    c = np.zeros((P, N_CONST), np.float32)
    for p in range(2):
        for part in range(2):
            for f in range(F):
                row = HS * p + F * part + f
                c[row, SEL1 + f * H:SEL1 + f * H + H] = 1
                for j in range(R0 // F):
                    c[row, SEL0 + F * j + f] = 1
                for n, shifts in enumerate(SHIFTS):
                    for j, shift in enumerate(shifts):
                        c[row, SEL0 + R0 * (1 + n) + F * j + (f - shift) % F] = 1
                c[row, SELT + F * p + f] = 1
    c[:, FOLD:FOLD + HS] = np.tile(np.eye(HS), (2, 1))
    c[:, IDENT:IDENT + P] = np.eye(P)
    c[:, MASK:MASK + GRP] = np.repeat(np.eye(GRP), D, axis=0)
    return c


def pair_rows(w):
    import numpy as np

    w = w.reshape(F, F, H)
    f = np.concatenate([np.arange(F) for s in SHIFTS for _ in s])
    g = np.concatenate([(np.arange(F) + shift) % F for s in SHIFTS for shift in s])
    return np.stack([w[f, g], w[g, f]])


_INS = ["dense_ctx", "ids"] + [f"tbl_{i}" for i in range(N_TABLES)] + [
    "W_top1", "b_top1", "W_top2", "b_top2", "W_top3", "L0_rec_W1", "L0_rec_W2"]


def kernel(**inputs):
    import numpy as _np
    import concourse.bacc as _bacc
    from concourse import mybir as _mybir
    from concourse.bass_utils import run_bass_kernel_spmd as _run

    nc = _bacc.Bacc("TRN2", target_bir_lowering=False, num_devices=1)
    arrays = {name: _np.ascontiguousarray(inputs[name]) for name in _INS}
    arrays["W0_pairs"] = _np.ascontiguousarray(pair_rows(_np.asarray(inputs["L0_rec_W0"])))
    arrays["consts"] = selections()
    tensors = {
        name: nc.dram_tensor(f"in_{name}_dram", a.shape, _mybir.dt.from_np(a.dtype), kind="ExternalInput").ap()
        for name, a in arrays.items()
    }
    out = nc.dram_tensor("out_0_dram", (B, 1), _mybir.dt.float32, kind="ExternalOutput").ap()
    cin_tower(nc, tensors, out)
    r = _run(nc, [{f"in_{name}_dram": a for name, a in arrays.items()}], core_ids=[0])
    return r.results[0]["out_0_dram"]
```

```python
from contextlib import ExitStack

import concourse.bass as bass
from concourse import mybir

ALU = mybir.AluOpType
ACT = mybir.ActivationFunctionType
F32 = mybir.dt.float32
BF16 = mybir.dt.bfloat16
I32 = mybir.dt.int32
AX_X = mybir.AxisListType.X

B, F, D, H = 1024, 24, 16, 64
N_TABLES = F
DENSE = 16
TOP1, TOP2 = 512, 256

P = 128
NBLK = B // P
HS = P // 2
NU = 2 * NBLK
DH = D // 2
NT = DH * HS
FP = 2
NC = F // FP
GRP = 8
NG = HS // GRP
GC = F + 1

SHIFTS = [[1, 2, 3, 4, 5], [6, 7, 8, 9, 10], [11, 0, 12]]
ROWS0 = [F * len(s) for s in SHIFTS]
BOTH = [ROWS0[0], ROWS0[1], F]
R0 = ROWS0[0]

NPART = 3
FR = NPART * F

SEL1 = 0
SEL0 = SEL1 + NC * P
SELT = SEL0 + 4 * R0
IDENT = SELT + F
MASK = IDENT + P
N_CONST = MASK + GRP

ORDER = ["c0", "c1", "c2", "c3", "c4", "a", "c5", "b0", "c6", "b1", "c7", "b2", "c8", "c9", "c10", "c11"]
A_PLACE = ORDER.index("a")
NUMBER = {w: n for n, w in enumerate(w for w in ORDER if w != "a")}
LAST = [w for w in ORDER if w[0] == "c"]
HEAD = ["a", "b0", "b1", "b2"]
NZ = 3


def cin_tower(nc, t, out):
    with ExitStack() as ctx:
        def sb(name, shape, dt=F32):
            return ctx.enter_context(nc.sbuf_tensor(name, shape, dt))

        def sem(name):
            return ctx.enter_context(nc.semaphore(name))

        ids_sb = sb("ids_sb", [P, NBLK * F], I32)
        idx = sb("idx", [P, F], I32)
        emb = sb("emb", [P, F, D])
        consts = sb("consts", [P, N_CONST])
        sel = sb("sel", [P, MASK], BF16)
        parts = sb("parts", [P, D, NPART, F], BF16)
        rest = sb("rest", [P, F, D])
        xp = sb("xp", [FR, P, D], BF16)
        a0 = sb("a0", [P, 2, NT])
        x1 = sb("x1", [P, 2, 2, NT])
        prod = sb("prod", [P, NZ, 2, NT])
        x2 = sb("x2", [P, HS, D])
        x2t = sb("x2t", [P, NG, P])
        bd = sb("bd", [P, NG, 2, GRP, GC])
        gram = sb("gram", [P, NC + 1, 2, HS])
        z1h = sb("z1h", [P, 2, HS])
        z3b = sb("z3b", [H, 2, HS])
        za = sb("za", [P, 2, NBLK * HS])
        zb = sb("zb", [H + DENSE, 2, NBLK * HS])
        w0 = sb("w0", [P, 3, H])
        w0t = sb("w0t", [P, 3, H])
        w1 = sb("w1", [P, NC, H])
        w2 = sb("w2", [P, NC, H])
        wt1a = sb("wt1a", [P, TOP1])
        wt1b = sb("wt1b", [H + DENSE, TOP1])
        wt2 = sb("wt2", [P, TOP1 // P, TOP2])
        wt3 = sb("wt3", [P, TOP2 // P])
        bt1 = sb("bt1", [P, TOP1 // P])
        bt2 = sb("bt2", [P, TOP2 // P])
        dense = sb("dense", [P, NBLK, DENSE])
        h1 = sb("h1", [P, TOP1 // P, 2, NBLK * HS])
        h2 = sb("h2", [P, TOP2 // P, 2, NBLK * HS])
        y = sb("y", [1, P, NBLK])

        ps = ctx.enter_context(nc.psum_tensor("ps", [P, 8, 512], F32))
        X1B, X2B, M0, M1 = 4, 5, 6, 7

        ids_loaded = sem("ids_loaded")
        consts_loaded = sem("consts_loaded")
        cin_loaded = sem("cin_loaded")
        dense_loaded = sem("dense_loaded")
        top_loaded = sem("top_loaded")
        idx_ready = sem("idx_ready")
        gathered = sem("gathered")
        sel_ready = sem("sel_ready")
        w0_ready = sem("w0_ready")
        bd_ones = sem("bd_ones")
        high_split = sem("high_split")
        rest_ready = sem("rest_ready")
        mid_split = sem("mid_split")
        low_split = sem("low_split")
        xp_ready = sem("xp_ready")
        xp_copied = sem("xp_copied")
        filled = sem("filled")
        a0_copied = sem("a0_copied")
        multiplied = sem("multiplied")
        summed = sem("summed")
        x1_copied = sem("x1_copied")
        z1_reduced = sem("z1_reduced")
        z1_added = sem("z1_added")
        x2_copied = sem("x2_copied")
        x0t_ready = sem("x0t_ready")
        bd_built = sem("bd_built")
        x2t_ready = sem("x2t_ready")
        x2t_copied = sem("x2t_copied")
        gram_ready = sem("gram_ready")
        gram_copied = sem("gram_copied")
        z2_copied = sem("z2_copied")
        z3_ready = sem("z3_ready")
        z3b_copied = sem("z3b_copied")
        z3_added = sem("z3_added")
        dense_turned = sem("dense_turned")
        dense_copied = sem("dense_copied")
        h1_ready = sem("h1_ready")
        h1_copied = sem("h1_copied")
        h2_ready = sem("h2_ready")
        h2_copied = sem("h2_copied")
        y_ready = sem("y_ready")
        y_copied = sem("y_copied")
        stored = sem("stored")

        ident = consts[:, IDENT:IDENT + P]
        mask = consts[:, MASK:MASK + GRP]

        def fills_before(u):
            return 4 + 16 * u

        def products_before(u):
            return 3 + 15 * u

        def slot(q):
            return 2 * (q % 2)

        block = ctx.enter_context(nc.Block())

        @block.sync
        def _(sp):
            sp.dma_start(ids_sb[:, :], t["ids"].rearrange("(s k) f -> s (k f)", k=NBLK)).then_inc(ids_loaded, 16)
            sp.dma_start(consts[:, :], t["consts"]).then_inc(consts_loaded, 16)
            for j, w in ((0, w0), (1, w0t)):
                sp.dma_start(w[0:R0, 0:2, :], t["W0_pairs"][j, 0:2 * R0, :].rearrange("(c r) o -> r c o", c=2)
                             ).then_inc(cin_loaded, 16)
                sp.dma_start(w[0:ROWS0[2], 2, :], t["W0_pairs"][j, 2 * R0:2 * R0 + ROWS0[2], :]
                             ).then_inc(cin_loaded, 16)
            sp.dma_start(w1[:, :, :], t["L0_rec_W1"].rearrange("(c r) o -> r c o", r=P)).then_inc(cin_loaded, 16)
            sp.dma_start(w2[:, :, :], t["L0_rec_W2"].rearrange("(c r) o -> r c o", r=P)).then_inc(cin_loaded, 16)
            sp.dma_start(dense[:, :, :], t["dense_ctx"].rearrange("(s k) c -> s k c", k=NBLK)).then_inc(dense_loaded, 16)
            for rows, src in ((slice(0, H), H), (slice(H, P), 0)):
                sp.dma_start(wt1a[rows, :], t["W_top1"][src:src + H, :]).then_inc(top_loaded, 16)
            sp.dma_start(wt1b[:, :], t["W_top1"][P:P + H + DENSE, :]).then_inc(top_loaded, 16)
            sp.dma_start(wt2[:, :, :], t["W_top2"].rearrange("(r c) m -> r c m", r=P)).then_inc(top_loaded, 16)
            sp.dma_start(wt3[:, :], t["W_top3"].rearrange("(r c) m -> r (c m)", r=P)).then_inc(top_loaded, 16)
            sp.dma_start(bt1[:, :], t["b_top1"].rearrange("(r c) -> r c", r=P)).then_inc(top_loaded, 16)
            sp.dma_start(bt2[:, :], t["b_top2"].rearrange("(r c) -> r c", r=P)).then_inc(top_loaded, 16)
            sp.wait_ge(y_copied, 2)
            sp.dma_start(out.rearrange("(a s) k -> a (s k)", a=1), y[:, :, :].rearrange("a s k -> a (s k)")
                         ).then_inc(stored, 16)
            sp.wait_ge(stored, 16)

        N_CIN, N_TOP = 6 * 16, 7 * 16

        @block.gpsimd
        def _(pool):
            def gather():
                for f in range(F):
                    pool.indirect_dma_start(emb[:, f, :], None, t[f"tbl_{f}"],
                                            bass.IndirectOffsetOnAxis(ap=idx[:, f:f + 1], axis=0)
                                            ).then_inc(gathered, 16)

            pool.wait_ge(ids_loaded, 16)
            pool.tensor_copy(idx[:, :], ids_sb[:, 0:F]).then_inc(idx_ready, 1)
            pool.wait_ge(idx_ready, 1)
            with pool.Fori(0, NBLK - 1) as k:
                gather()
                pool.wait_ge(low_split, k + 1)
                pool.tensor_copy(idx[:, :], ids_sb[:, bass.ds(k * F + F, F)]).then_inc(idx_ready, 1)
                pool.wait_ge(idx_ready, k + 2)
            gather()

        @block.scalar
        def _(act):
            def split_high(k):
                act.wait_ge(gathered, (k + 1) * (16 * F))
                act.wait_ge(xp_ready, 2 * k)
                nc.scalar.activation(parts[:, :, 0, :], emb[:, :, :].rearrange("s f d -> s d f"),
                                     ACT.Copy).then_inc(high_split, 1)

            def split_mid(k):
                act.wait_ge(rest_ready, k + 1)
                nc.scalar.activation(parts[:, :, 1, :], rest[:, :, :].rearrange("s f d -> s d f"),
                                     ACT.Copy).then_inc(mid_split, 1)

            def copy_xp(k, h):
                act.wait_ge(xp_ready, 2 * k + h + 1)
                nc.scalar.activation(xp[:, :, DH * h:DH * h + DH].rearrange("r s d -> r d s"),
                                     ps[0:FR, M1, :].bitcast(BF16).rearrange("r (d s) -> r d s", s=P),
                                     ACT.Copy).then_inc(xp_copied, 1)

            def copy_a0(u, n, q):
                act.wait_ge(filled, n + 1)
                s = slot(q)
                nc.scalar.activation(a0[0:R0, :, :], ps[0:R0, s:s + 2, :], ACT.Copy).then_inc(a0_copied, 1)

            def copy_x1(u, par, head=False):
                act.wait_ge(summed, products_before(u - 1) + NUMBER["b2"] + 1 if not head else 3)
                for twice in range(2):
                    for p in range(2):
                        ins = nc.scalar.activation(x1[HS * twice:HS * twice + H, par, p, :],
                                                   ps[HS * p:HS * p + H, X1B, :], ACT.Copy)
                ins.then_inc(x1_copied, 1)

            def copy_x2(u, h, last=False):
                act.wait_ge(summed, products_before(u) + (NC if last else len(NUMBER)))
                nc.scalar.activation(x2[:, :, DH * h:DH * h + DH], ps[:, X2B, :].rearrange("r (s d) -> r s d", d=DH),
                                     ACT.Copy).then_inc(x2_copied, 1)

            def build_bd(k):
                act.wait_ge(x0t_ready, k + 1)
                for j in range(GRP):
                    ins = nc.scalar.activation(bd[:, :, :, j, 0:F].rearrange("r g p f -> r (g p) f"),
                                               ps[:, M0, 0:NG * 2 * F].rearrange("r (a f) -> r a f", f=F),
                                               ACT.Copy, scale=mask[:, j:j + 1])
                ins.then_inc(bd_built, 1)

            def copy_x2t(k, j):
                act.wait_ge(x2t_ready, 2 * k + j + 1)
                nc.scalar.activation(x2t[:, 4 * j:4 * j + 4, :].rearrange("r g c -> r (g c)"), ps[:, M0 + j, :],
                                     ACT.Copy).then_inc(x2t_copied, 1)

            def copy_gram(k, j):
                act.wait_ge(gram_ready, 4 * k + j + 1)
                n = 2 * GRP
                for p in range(2):
                    g = ps[HS * p:HS * p + H, M0 + j % 2, 0:n * GC].rearrange("r (s f) -> r s f", f=GC)
                    for f2 in range(FP):
                        ins = nc.scalar.activation(
                            gram[H * f2:H * f2 + H, 0:NC + 1 - f2, p, n * j:n * j + n].rearrange("r f s -> r s f"),
                            g[:, :, f2:GC:FP], ACT.Copy)
                ins.then_inc(gram_copied, 1)

            def copy_z2(k):
                act.wait_ge(gram_copied, 4 * k + 4)
                nc.scalar.activation(za[0:H, :, bass.ds(k * HS, HS)], gram[0:H, NC, :, :], ACT.Copy
                                     ).then_inc(z2_copied, 1)

            def copy_z3b(k):
                act.wait_ge(z3_ready, k + 1)
                nc.scalar.activation(z3b[:, :, :].rearrange("o p s -> o (p s)"), ps[H:P, M0, 0:P], ACT.Copy
                                     ).then_inc(z3b_copied, 1)

            act.wait_ge(consts_loaded, 16)
            act.wait_ge(dense_turned, 1)
            for p in range(2):
                ins = nc.scalar.activation(
                    zb[H:H + DENSE, p, :].rearrange("c (k s) -> c k s", s=HS),
                    ps[0:DENSE, X1B:X1B + 2, :].rearrange("c b (k s) -> c (b k) s", s=P)[:, :, HS * p:HS * p + HS],
                    ACT.Copy)
            ins.then_inc(dense_copied, 1)
            split_high(0)
            split_mid(0)
            copy_xp(0, 0)
            copy_a0(0, 0, 0)
            copy_x1(0, 0, head=True)

            def odd_step(u, k, last=False):
                copy_x2(u - 1, 0)
                if not last:
                    split_high(k + 1)
                    split_mid(k + 1)
                    copy_xp(k + 1, 0)
                    copy_a0(u + 1, fills_before(u) + A_PLACE, A_PLACE)
                build_bd(k)
                if not last:
                    copy_x1(u + 1, 0)

            def even_step(u, k, first=False):
                if not first:
                    copy_x2(u - 1, 1)
                copy_xp(k, 1)
                if not first:
                    copy_x2t(k - 1, 0)
                    copy_x2t(k - 1, 1)
                copy_a0(u + 1, fills_before(u) + A_PLACE, A_PLACE)
                if not first:
                    for j in range(4):
                        copy_gram(k - 1, j)
                copy_x1(u + 1, 1)
                if not first:
                    copy_z2(k - 1)
                    copy_z3b(k - 1)

            even_step(0, 0, first=True)
            with act.Fori(0, NBLK - 1) as i:
                odd_step(2 * i + 1, i)
                even_step(2 * i + 2, i + 1)
            odd_step(NU - 1, NBLK - 1, last=True)
            copy_x2(NU - 1, 1, last=True)
            for j in range(2):
                copy_x2t(NBLK - 1, j)
            for j in range(4):
                copy_gram(NBLK - 1, j)
            copy_z2(NBLK - 1)
            copy_z3b(NBLK - 1)

            act.wait_ge(top_loaded, N_TOP)
            for m in range(TOP1 // P):
                act.wait_ge(h1_ready, m + 1)
                for p in range(2):
                    ins = nc.scalar.activation(h1[:, m, p, :], ps[:, 2 * m + p, :], ACT.Relu, bias=bt1[:, m:m + 1])
                ins.then_inc(h1_copied, 1)
            for m in range(TOP2 // P):
                act.wait_ge(h2_ready, m + 1)
                for p in range(2):
                    ins = nc.scalar.activation(h2[:, m, p, :], ps[:, 2 * m + p, :], ACT.Relu, bias=bt2[:, m:m + 1])
                ins.then_inc(h2_copied, 1)
            for p in range(2):
                act.wait_ge(y_ready, p + 1)
                nc.scalar.activation(y[:, HS * p:HS * p + HS, :],
                                     ps[0:1, 4 + p, :].rearrange("a (k s) -> a s k", k=NBLK),
                                     ACT.Copy).then_inc(y_copied, 1)

        @block.vector
        def _(dve):
            def split_rest(k):
                dve.wait_ge(high_split, k + 1)
                nc.vector.tensor_tensor(rest[:, :, :].rearrange("s f d -> s d f"),
                                        emb[:, :, :].rearrange("s f d -> s d f"), parts[:, :, 0, :],
                                        ALU.subtract).then_inc(rest_ready, 1)

            def split_low(k):
                dve.wait_ge(mid_split, k + 1)
                nc.vector.tensor_tensor(parts[:, :, 2, :], rest[:, :, :].rearrange("s f d -> s d f"),
                                        parts[:, :, 1, :], ALU.subtract).then_inc(low_split, 1)

            def multiply(what, par, nfill, nprod, q, n):
                dve.wait_ge(filled, nfill + 1)
                if n >= NZ:
                    dve.wait_ge(summed, nprod - NZ + 1)
                rows = P if what[0] == "c" else ROWS0[int(what[1])]
                other = x1[0:rows, par, :, :] if what[0] == "c" else a0[0:rows, :, :]
                nc.vector.tensor_tensor(prod[0:rows, n % NZ, :, :], ps[0:rows, slot(q):slot(q) + 2, :], other,
                                        ALU.mult).then_inc(multiplied, 1)

            def reduce_z1(u, h):
                dve.wait_ge(x1_copied, u + 1)
                nc.vector.tensor_reduce(z1h[:, h, :], ps[:, X1B, :].rearrange("r (s d) -> r s d", d=DH), AX_X, ALU.add
                                        ).then_inc(z1_reduced, 1)

            def add_z1(u, k):
                dve.wait_ge(z1_reduced, u + 1)
                for p in range(2):
                    rows = slice(HS * p, HS * p + H)
                    ins = nc.vector.tensor_tensor(za[H:P, p, bass.ds(k * HS, HS)], z1h[rows, 0, :], z1h[rows, 1, :],
                                                  ALU.add)
                ins.then_inc(z1_added, 1)

            def add_z3(k):
                dve.wait_ge(z3b_copied, k + 1)
                nc.vector.tensor_tensor(zb[0:H, :, bass.ds(k * HS, HS)],
                                        ps[0:H, M0, 0:P].rearrange("o (p s) -> o p s", p=2), z3b[:, :, :],
                                        ALU.add).then_inc(z3_added, 1)

            def step(u, k, par, first=False, last=False):
                order = [w for w in (LAST if last else ORDER)]
                n = 0
                for q, what in enumerate(order):
                    if what == "a":
                        continue
                    if what == "c0":
                        dve.wait_ge(x1_copied, u + 1)
                    if what == "b0":
                        dve.wait_ge(a0_copied, u + 2)
                    multiply(what, par, fills_before(u) + q, products_before(u) + n, q, NZ + n)
                    n += 1
                    if q == 0:
                        reduce_z1(u, par)
                    if q == 1 and par == 1 and not last:
                        split_rest(k + 1)
                    if q == 2 and par == 1 and not last:
                        split_low(k + 1)
                    if q == 3 and par == 1:
                        add_z1(u, k)
                if par == 0 and not first:
                    add_z3(k - 1)

            dve.wait_ge(consts_loaded, 16)
            nc.vector.tensor_copy(sel[:, :], consts[:, 0:MASK]).then_inc(sel_ready, 1)
            nc.vector.tensor_copy(bd[:, :, :, :, F].rearrange("r g p j -> r (g p) j"),
                                  mask.unsqueeze(1).to_broadcast([P, 2 * NG, GRP])).then_inc(bd_ones, 1)
            dve.wait_ge(cin_loaded, N_CIN)
            for c in range(3):
                ins = nc.vector.tensor_tensor(w0[0:BOTH[c], c, :], w0[0:BOTH[c], c, :], w0t[0:BOTH[c], c, :], ALU.add)
            ins.then_inc(w0_ready, 1)
            split_rest(0)
            split_low(0)
            dve.wait_ge(a0_copied, 1)
            for j in range(3):
                multiply(f"b{j}", 0, 1 + j, j, 1 + j, j)
            step(0, 0, 0, first=True)
            with dve.Fori(0, NBLK - 1) as i:
                step(2 * i + 1, i, 1)
                step(2 * i + 2, i + 1, 0)
            step(NU - 1, NBLK - 1, 1, last=True)
            add_z3(NBLK - 1)

        @block.tensor
        def _(pe):
            def fill(what, q, h, free):
                s = slot(q)
                if free is not None:
                    pe.wait_ge(*free)
                if what[0] == "c":
                    col, m = SEL1 + int(what[1:]) * P, P
                else:
                    j = 0 if what == "a" else 1 + int(what[1])
                    col, m = SEL0 + j * R0, R0 if what == "a" else ROWS0[j - 1]
                for p in range(2):
                    ins = nc.tensor.matmul(ps[0:m, s + p, :], sel[0:FR, col:col + m],
                                           xp[:, HS * p:HS * p + HS, DH * h:DH * h + DH],
                                           start=True, stop=True)
                ins.then_inc(filled, 1)

            def contract(what, nprod, n):
                pe.wait_ge(multiplied, nprod + 1)
                j = int(what[1:])
                if what[0] == "c":
                    rows, w, bank, end = P, w1[:, j, :], X2B, NC - 1
                else:
                    rows, w, bank, end = ROWS0[j], w0[0:ROWS0[j], j, :], X1B, 2
                for p in range(2):
                    ins = nc.tensor.matmul(ps[HS * p:HS * p + H, bank, :], w, prod[0:rows, n % NZ, p, :],
                                           start=j == 0, stop=j == end)
                ins.then_inc(summed, 1)

            def build_xp(k, h):
                turned = ps[0:FR, M1, :].bitcast(BF16)
                for d in range(DH):
                    ins = nc.tensor.transpose(turned[:, P * d:P * d + P],
                                              parts[:, DH * h + d, :, :].rearrange("s n f -> s (n f)"),
                                              sel[:, IDENT:IDENT + P])
                ins.then_inc(xp_ready, 1)

            def turn_x0(k):
                for g in range(NG):
                    for p in range(2):
                        c = F * (2 * g + p)
                        s = HS * p + GRP * g
                        ins = nc.tensor.matmul(ps[:, M0, c:c + F], xp[:, s:s + GRP, :].rearrange("r s d -> r (s d)"),
                                               sel[0:FR, SELT:SELT + F], start=True, stop=True)
                ins.then_inc(x0t_ready, 1)

            def turn_x2(k, j):
                for g in range(4):
                    gg = 4 * j + g
                    ins = nc.tensor.transpose(ps[:, M0 + j, P * g:P * g + P], x2[:, GRP * gg:GRP * gg + GRP, :].rearrange("r s d -> r (s d)"), ident)
                ins.then_inc(x2t_ready, 1)

            def grams(k, j):
                n = GRP * GC
                for g in range(2):
                    gg = 2 * j + g
                    for p in range(2):
                        ins = nc.tensor.matmul(ps[HS * p:HS * p + H, M0 + j % 2, n * g:n * g + n],
                                               x2t[:, gg, HS * p:HS * p + H],
                                               bd[:, gg, p, :, :].rearrange("r j f -> r (j f)"), start=True, stop=True)
                ins.then_inc(gram_ready, 1)

            def layer3(c0, c1):
                half = NC // 2
                for c in range(c0, c1):
                    for n in range(2):
                        ins = nc.tensor.matmul(ps[H * n:H * n + H, M0, 0:P], w2[:, c + half * n, :],
                                               gram[:, c + half * n, :, :].rearrange("r p s -> r (p s)"),
                                               start=c == 0, stop=c == half - 1)
                if c1 == half:
                    ins.then_inc(z3_ready, 1)

            def gram_extra(k, q, tail=False):
                if q == 3:
                    pe.wait_ge(x2_copied, 2 * k + 2)
                    pe.wait_ge(bd_built, k + 1)
                    turn_x2(k, 0)
                if q == 4:
                    if not tail:
                        pe.wait_ge(xp_copied, 2 * k + 4)
                    turn_x2(k, 1)
                if q == 6:
                    pe.wait_ge(x2t_copied, 2 * k + 1)
                    grams(k, 0)
                if q == 7:
                    pe.wait_ge(x2t_copied, 2 * k + 2)
                    grams(k, 1)
                if q == 9:
                    pe.wait_ge(gram_copied, 4 * k + 1)
                    grams(k, 2)
                if q == 11:
                    pe.wait_ge(gram_copied, 4 * k + 2)
                    grams(k, 3)
                if q == 13:
                    if tail:
                        pe.wait_ge(gram_copied, 4 * k + 4)
                    layer3(0, 3)
                if q == 14:
                    layer3(3, 6)

            def extra(k, par, q, first, last):
                if par == 0:
                    if q == 1:
                        pe.wait_ge(xp_copied, 2 * k + 1)
                        build_xp(k, 1)
                    if not first:
                        gram_extra(k - 1, q)
                else:
                    if q == 2:
                        pe.wait_ge(xp_copied, 2 * k + 2)
                        turn_x0(k)
                    if q == 4 and not last:
                        pe.wait_ge(low_split, k + 2)
                        build_xp(k + 1, 0)

            def step(u, k, par, first=False, last=False):
                order = LAST if last else ORDER
                filled_so_far = (HEAD if first else ORDER)[-2:] + order
                for q, what in enumerate(order):
                    old = filled_so_far[q]
                    if q < 2:
                        number = q - 2
                    elif old != "a":
                        number = NUMBER[old] if not last else q - 2
                    if what == "a":
                        pe.wait_ge(xp_copied, 2 * k + 2 + par)
                    if q == 13 and par == 0 and not first:
                        pe.wait_ge(gram_copied, 4 * k)
                    if old == "a":
                        fill(what, q, 1 - par if what[0] != "c" else par, (a0_copied, u + 2))
                    else:
                        fill(what, q, 1 - par if what[0] != "c" else par, (multiplied, products_before(u) + number + 1))
                        if old == "c0" and not first:
                            pe.wait_ge(x2_copied, u)
                        if old == "b0":
                            pe.wait_ge(z1_reduced, u + 1)
                        contract(old, products_before(u) + number, NZ + number)
                    extra(k, par, q, first, last)

            pe.wait_ge(consts_loaded, 16)
            pe.wait_ge(dense_loaded, 16)
            for k in range(NBLK):
                ins = nc.tensor.transpose(ps[0:DENSE, X1B + k // 4, P * (k % 4):P * (k % 4) + P], dense[:, k, :], ident)
            ins.then_inc(dense_turned, 1)
            pe.wait_ge(sel_ready, 1)
            pe.wait_ge(low_split, 1)
            build_xp(0, 0)
            pe.wait_ge(xp_copied, 1)
            pe.wait_ge(w0_ready, 1)
            pe.wait_ge(cin_loaded, N_CIN)
            pe.wait_ge(bd_ones, 1)
            pe.wait_ge(dense_copied, 1)
            fill("a", 0, 0, None)
            fill("b0", 1, 0, None)
            fill("b1", 2, 0, (a0_copied, 1))
            fill("b2", 3, 0, (multiplied, 1))
            contract("b0", 0, 0)
            step(0, 0, 0, first=True)
            with pe.Fori(0, NBLK - 1) as i:
                step(2 * i + 1, i, 1)
                step(2 * i + 2, i + 1, 0)
            step(NU - 1, NBLK - 1, 1, last=True)
            done = products_before(NU - 1) + NC
            for n in (NC - 2, NC - 1):
                contract(f"c{n}", done - NC + n, NZ + n)
            for q in range(len(ORDER)):
                gram_extra(NBLK - 1, q, tail=True)

            pe.wait_ge(top_loaded, N_TOP)
            pe.wait_ge(z3_added, NBLK)
            pe.wait_ge(z2_copied, NBLK)
            pe.wait_ge(z1_added, NBLK)
            for m in range(TOP1 // P):
                cols = slice(m, TOP1, TOP1 // P)
                for w, x, start in ((wt1a, za, True), (wt1b, zb, False)):
                    for p in range(2):
                        ins = nc.tensor.matmul(ps[:, 2 * m + p, :], w[:, cols], x[:, p, :], start=start, stop=not start)
                ins.then_inc(h1_ready, 1)
            for m in range(TOP2 // P):
                for c in range(TOP1 // P):
                    pe.wait_ge(h1_copied, c + 1)
                    for p in range(2):
                        ins = nc.tensor.matmul(ps[:, 2 * m + p, :], wt2[:, c, m:TOP2:TOP2 // P], h1[:, c, p, :],
                                               start=c == 0, stop=c == TOP1 // P - 1)
                ins.then_inc(h2_ready, 1)
            for p in range(2):
                for c in range(TOP2 // P):
                    pe.wait_ge(h2_copied, c + 1)
                    ins = nc.tensor.matmul(ps[0:1, 4 + p, :], wt3[:, c:c + 1], h2[:, c, p, :],
                                           start=c == 0, stop=c == TOP2 // P - 1)
                ins.then_inc(y_ready, 1)


def selections():
    import numpy as np

    c = np.zeros((P, N_CONST), np.float32)
    for part in range(NPART):
        for f in range(F):
            row = F * part + f
            c[row, SEL1 + f * H:SEL1 + f * H + H] = 1
            for j in range(R0 // F):
                c[row, SEL0 + F * j + f] = 1
            for n, shifts in enumerate(SHIFTS):
                for j, shift in enumerate(shifts):
                    c[row, SEL0 + R0 * (1 + n) + F * j + (f - shift) % F] = 1
            c[row, SELT + f] = 1
    c[:, IDENT:IDENT + P] = np.eye(P)
    c[:, MASK:MASK + GRP] = np.repeat(np.eye(GRP), D, axis=0)
    return c


def pair_rows(w):
    import numpy as np

    w = w.reshape(F, F, H)
    f = np.concatenate([np.arange(F) for s in SHIFTS for _ in s])
    g = np.concatenate([(np.arange(F) + shift) % F for s in SHIFTS for shift in s])
    return np.stack([w[f, g], w[g, f]])


_INS = ["dense_ctx", "ids"] + [f"tbl_{i}" for i in range(N_TABLES)] + [
    "W_top1", "b_top1", "W_top2", "b_top2", "W_top3", "L0_rec_W1", "L0_rec_W2"]


def kernel(**inputs):
    import numpy as _np
    import concourse.bacc as _bacc
    from concourse import mybir as _mybir
    from concourse.bass_utils import run_bass_kernel_spmd as _run

    nc = _bacc.Bacc("TRN2", target_bir_lowering=False, num_devices=1)
    arrays = {name: _np.ascontiguousarray(inputs[name]) for name in _INS}
    arrays["W0_pairs"] = _np.ascontiguousarray(pair_rows(_np.asarray(inputs["L0_rec_W0"])))
    arrays["consts"] = selections()
    tensors = {
        name: nc.dram_tensor(f"in_{name}_dram", a.shape, _mybir.dt.from_np(a.dtype), kind="ExternalInput").ap()
        for name, a in arrays.items()
    }
    out = nc.dram_tensor("out_0_dram", (B, 1), _mybir.dt.float32, kind="ExternalOutput").ap()
    cin_tower(nc, tensors, out)
    r = _run(nc, [{f"in_{name}_dram": a for name, a in arrays.items()}], core_ids=[0])
    return r.results[0]["out_0_dram"]
```

```python
from contextlib import ExitStack

import concourse.bass as bass
from concourse import mybir

ALU = mybir.AluOpType
ACT = mybir.ActivationFunctionType
F32 = mybir.dt.float32
BF16 = mybir.dt.bfloat16
I32 = mybir.dt.int32
AX_X = mybir.AxisListType.X

B, F, D, H = 1024, 24, 16, 64
N_TABLES = F
DENSE = 16
TOP1, TOP2 = 512, 256

P = 128
NBLK = B // P
HS = P // 2
NU = 2 * NBLK
DH = D // 2
NT = DH * HS
FP = 2
NC = F // FP
GRP = 8
NG = HS // GRP
GC = F + 1

SHIFTS = [[1, 2, 3, 4, 5], [6, 7, 8, 9, 10], [11, 0, 12]]
ROWS0 = [F * len(s) for s in SHIFTS]
BOTH = [ROWS0[0], ROWS0[1], F]
R0 = ROWS0[0]

NPART = 3
FR = NPART * F

SEL1 = 0
SEL0 = SEL1 + NC * P
SELT = SEL0 + 4 * R0
IDENT = SELT + F
MASK = IDENT + P
N_CONST = MASK + GRP

ORDER = ["c0", "c1", "c2", "c3", "c4", "c5", "a", "b0", "c6", "b1", "b2", "c7", "c8", "c9", "c10", "c11"]
GROUPS = [["c1", "c2"], ["c4", "c5"], ["c6", "c7", "c8"], ["c9", "c10", "c11"]]
SPREAD = [w for group in GROUPS for w in group]
LAST = [w for w in ORDER if w[0] == "c"]
HEAD = ["a", "b0", "b1", "b2"]


def numbers(order):
    return {w: n for n, w in enumerate(w for w in order if w != "a")}


def ring_numbers(order):
    return {w: n for n, w in enumerate(w for w in order if w not in SPREAD)}


NUMBER, RING = numbers(ORDER), ring_numbers(ORDER)
NZ = 5
LAG = 3

WARM_FROM = 19
WARM = {"gathers": 24, "xp": 4, "a0": 2, "b0": 2, "b1": 2, "x1": 8}


def cin_tower(nc, t, out):
    with ExitStack() as ctx:
        def sb(name, shape, dt=F32):
            return ctx.enter_context(nc.sbuf_tensor(name, shape, dt))

        def sem(name):
            return ctx.enter_context(nc.semaphore(name))

        ids_sb = sb("ids_sb", [P, NBLK * F], I32)
        idx = sb("idx", [P, F], I32)
        emb = sb("emb", [P, F, D])
        tick = sb("tick", [1, 1])
        consts = sb("consts", [P, N_CONST])
        sel = sb("sel", [P, MASK], BF16)
        parts = sb("parts", [P, D, NPART, F], BF16)
        rest = sb("rest", [P, F, D])
        xp = sb("xp", [FR, P, D], BF16)
        a0 = sb("a0", [P, 2, NT])
        x1 = sb("x1", [P, 2, 2, NT])
        ab = sb("ab", [P, len(SPREAD), 2 * NT])
        prod = sb("prod", [P, NZ, 2, NT])
        x2 = sb("x2", [P, HS, D])
        x2t = sb("x2t", [P, NG, P])
        bd = sb("bd", [P, NG, 2, GRP, GC])
        gram = sb("gram", [P, NC + 1, 2, HS])
        z1h = sb("z1h", [P, 2, HS])
        z3b = sb("z3b", [H, P])
        za = sb("za", [P, B])
        zb = sb("zb", [H + DENSE, B])
        w0 = sb("w0", [P, 3, H])
        w0t = sb("w0t", [P, 3, H])
        w1 = sb("w1", [P, NC, H])
        w2 = sb("w2", [P, NC, H])
        wt1a = sb("wt1a", [P, TOP1])
        wt1b = sb("wt1b", [H + DENSE, TOP1])
        wt2 = sb("wt2", [P, TOP1 // P, TOP2])
        wt3 = sb("wt3", [P, TOP2 // P])
        bt1 = sb("bt1", [P, TOP1 // P])
        bt2 = sb("bt2", [P, TOP2 // P])
        dense = sb("dense", [P, NBLK, DENSE])
        h1 = sb("h1", [P, TOP1 // P, B])
        h2 = sb("h2", [P, TOP2 // P, B])
        y = sb("y", [P, NBLK])

        ps = ctx.enter_context(nc.psum_tensor("ps", [P, 8, 512], F32))
        X1B, X2B, M0, M1 = 4, 5, 6, 7

        ids_loaded = sem("ids_loaded")
        consts_loaded = sem("consts_loaded")
        cin_loaded = sem("cin_loaded")
        dense_loaded = sem("dense_loaded")
        top_loaded = sem("top_loaded")
        idx_ready = sem("idx_ready")
        gathered = sem("gathered")
        nearly_gathered = sem("nearly_gathered")
        sel_ready = sem("sel_ready")
        w0_ready = sem("w0_ready")
        bd_ones = sem("bd_ones")
        high_split = sem("high_split")
        rest_ready = sem("rest_ready")
        mid_split = sem("mid_split")
        low_split = sem("low_split")
        xp_ready = sem("xp_ready")
        xp_copied = sem("xp_copied")
        filled = sem("filled")
        a0_copied = sem("a0_copied")
        x0_stored = sem("x0_stored")
        spread = [sem(f"spread_{n}") for n in range(len(GROUPS))]
        shared = sem("shared")
        multiplied = sem("multiplied")
        summed = sem("summed")
        x1_copied = sem("x1_copied")
        z1_reduced = sem("z1_reduced")
        z1_added = sem("z1_added")
        x2_copied = sem("x2_copied")
        x0t_ready = sem("x0t_ready")
        bd_built = sem("bd_built")
        x2t_ready = sem("x2t_ready")
        x2t_copied = sem("x2t_copied")
        gram_ready = sem("gram_ready")
        gram_copied = sem("gram_copied")
        z2_copied = sem("z2_copied")
        z3_ready = sem("z3_ready")
        z3b_copied = sem("z3b_copied")
        z3_added = sem("z3_added")
        dense_turned = sem("dense_turned")
        dense_copied = sem("dense_copied")
        h1_ready = sem("h1_ready")
        h1_copied = sem("h1_copied")
        h2_ready = sem("h2_ready")
        h2_copied = sem("h2_copied")
        y_ready = sem("y_ready")
        y_copied = sem("y_copied")
        stored = sem("stored")

        ident = consts[:, IDENT:IDENT + P]
        mask = consts[:, MASK:MASK + GRP]

        def fills_before(u):
            return len(HEAD) + len(RING) * u

        def products_before(u):
            return len(HEAD) - 1 + len(NUMBER) * u

        def slot(r):
            return 2 * (r % 2)

        def head_xp(share):
            d = DH // 2 * share
            return (xp[:, :, d:d + DH // 2].rearrange("r s d -> r d s"),
                    ps[0:FR, M0 + share, 0:P * DH // 4].bitcast(BF16).rearrange("r (d s) -> r d s", s=P))

        def head_a0(share):
            return a0[0:R0, share, :], ps[0:R0, share, :]

        def head_x1(twice, p):
            return x1[HS * twice:HS * twice + H, 0, p, :], ps[HS * p:HS * p + H, X1B, :]

        block = ctx.enter_context(nc.Block())

        @block.sync
        def _(sp):
            sp.dma_start(ids_sb[:, :], t["ids"].rearrange("(s k) f -> s (k f)", k=NBLK)).then_inc(ids_loaded, 16)
            sp.dma_start(consts[:, :], t["consts"]).then_inc(consts_loaded, 16)
            for j, w in ((0, w0), (1, w0t)):
                sp.dma_start(w[0:R0, 0:2, :], t["W0_pairs"][j, 0:2 * R0, :].rearrange("(c r) o -> r c o", c=2)
                             ).then_inc(cin_loaded, 16)
                sp.dma_start(w[0:ROWS0[2], 2, :], t["W0_pairs"][j, 2 * R0:2 * R0 + ROWS0[2], :]
                             ).then_inc(cin_loaded, 16)
            sp.dma_start(w1[:, :, :], t["L0_rec_W1"].rearrange("(c r) o -> r c o", r=P)).then_inc(cin_loaded, 16)
            sp.dma_start(w2[:, :, :], t["L0_rec_W2"].rearrange("(c r) o -> r c o", r=P)).then_inc(cin_loaded, 16)
            sp.dma_start(dense[:, :, :], t["dense_ctx"].rearrange("(s k) c -> s k c", k=NBLK)).then_inc(dense_loaded, 16)
            for rows, src in ((slice(0, H), H), (slice(H, P), 0)):
                sp.dma_start(wt1a[rows, :], t["W_top1"][src:src + H, :]).then_inc(top_loaded, 16)
            sp.dma_start(wt1b[:, :], t["W_top1"][P:P + H + DENSE, :]).then_inc(top_loaded, 16)
            sp.dma_start(wt2[:, :, :], t["W_top2"].rearrange("(r c) m -> r c m", r=P)).then_inc(top_loaded, 16)
            sp.dma_start(wt3[:, :], t["W_top3"].rearrange("(r c) m -> r (c m)", r=P)).then_inc(top_loaded, 16)
            sp.dma_start(bt1[:, :], t["b_top1"].rearrange("(r c) -> r c", r=P)).then_inc(top_loaded, 16)
            sp.dma_start(bt2[:, :], t["b_top2"].rearrange("(r c) -> r c", r=P)).then_inc(top_loaded, 16)

            def spread_x0(u, par, first=False):
                sp.wait_ge(a0_copied, u + 1)
                sp.dma_start(t["x0d"][par, :, :, :].rearrange("c f n -> (c f) n"),
                             a0[0:F, :, :].rearrange("f p n -> f (p n)")).then_inc(x0_stored, 16)
                sp.wait_ge(x0_stored, 16 * u + 16)
                for n, group in enumerate(GROUPS):
                    if not first and n > 0:
                        sp.wait_ge(multiplied, products_before(u - 1) + NUMBER[group[-1]] + 1)
                    j, c = SPREAD.index(group[0]), int(group[0][1:])
                    for f2 in range(FP):
                        sp.dma_start(ab[H * f2:H * f2 + H, j:j + len(group), :],
                                     t["x0d"][par:par + 1, c:c + len(group), f2, :].to_broadcast([H, len(group), 2 * NT])
                                     ).then_inc(spread[n], 16)

            sp.wait_ge(shared, 2)
            spread_x0(0, 0, first=True)
            with sp.Fori(0, NBLK - 1) as i:
                spread_x0(2 * i + 1, 1)
                spread_x0(2 * i + 2, 0)
            spread_x0(NU - 1, 1)
            sp.wait_ge(y_copied, 1)
            sp.dma_start(out.rearrange("(s k) a -> s (k a)", k=NBLK), y[:, :]).then_inc(stored, 16)
            sp.wait_ge(stored, 16)

        N_CIN, N_TOP = 6 * 16, 7 * 16

        @block.gpsimd
        def _(pool):
            def gather(ids, first=False):
                for f in range(F):
                    if first and f == WARM_FROM:
                        pool.memset(tick[:, :], 0.0).then_inc(nearly_gathered, 1)
                    pool.indirect_dma_start(emb[:, f, :], None, t[f"tbl_{f}"],
                                            bass.IndirectOffsetOnAxis(ap=ids[:, f:f + 1], axis=0)
                                            ).then_inc(gathered, 16)

            pool.wait_ge(ids_loaded, 16)
            gather(ids_sb, first=True)
            pool.wait_ge(low_split, 1)
            pool.tensor_copy(idx[:, :], ids_sb[:, F:2 * F]).then_inc(idx_ready, 1)
            pool.wait_ge(idx_ready, 1)
            with pool.Fori(1, NBLK - 1) as k:
                gather(idx)
                pool.wait_ge(low_split, k + 1)
                pool.tensor_copy(idx[:, :], ids_sb[:, bass.ds(k * F + F, F)]).then_inc(idx_ready, 1)
                pool.wait_ge(idx_ready, k + 1)
            gather(idx)

        @block.scalar
        def _(act):
            def split_high(k):
                act.wait_ge(gathered, (k + 1) * (16 * F))
                if not isinstance(k, int) or k > 0:
                    act.wait_ge(xp_ready, 2 * k)
                nc.scalar.activation(parts[:, :, 0, :], emb[:, :, :].rearrange("s f d -> s d f"),
                                     ACT.Copy).then_inc(high_split, 1)

            def split_mid(k):
                act.wait_ge(rest_ready, k + 1)
                nc.scalar.activation(parts[:, :, 1, :], rest[:, :, :].rearrange("s f d -> s d f"),
                                     ACT.Copy).then_inc(mid_split, 1)

            def copy_xp(k, h):
                act.wait_ge(xp_ready, 2 * k + h + 1)
                nc.scalar.activation(xp[:, :, DH * h:DH * h + DH].rearrange("r s d -> r d s"),
                                     ps[0:FR, M1, :].bitcast(BF16).rearrange("r (d s) -> r d s", s=P),
                                     ACT.Copy).then_inc(xp_copied, 1)

            def copy_a0(u, n, r):
                act.wait_ge(filled, n + 1)
                s = slot(r)
                nc.scalar.activation(a0[0:R0, :, :], ps[0:R0, s:s + 2, :], ACT.Copy).then_inc(a0_copied, 1)

            def copy_x1(u, par):
                act.wait_ge(summed, products_before(u - 1) + NUMBER["b2"] + 1)
                for twice in range(2):
                    for p in range(2):
                        ins = nc.scalar.activation(x1[HS * twice:HS * twice + H, par, p, :],
                                                   ps[HS * p:HS * p + H, X1B, :], ACT.Copy)
                ins.then_inc(x1_copied, 1)

            def copy_x2(u, h, last=False):
                act.wait_ge(summed, products_before(u) + (NC if last else len(NUMBER)))
                nc.scalar.activation(x2[:, :, DH * h:DH * h + DH], ps[:, X2B, :].rearrange("r (s d) -> r s d", d=DH),
                                     ACT.Copy).then_inc(x2_copied, 1)

            def build_bd(k):
                act.wait_ge(x0t_ready, k + 1)
                for j in range(GRP):
                    ins = nc.scalar.activation(bd[:, :, :, j, 0:F].rearrange("r g p f -> r (g p) f"),
                                               ps[:, M0, 0:NG * 2 * F].rearrange("r (a f) -> r a f", f=F),
                                               ACT.Copy, scale=mask[:, j:j + 1])
                ins.then_inc(bd_built, 1)

            def copy_x2t(k, j):
                act.wait_ge(x2t_ready, 2 * k + j + 1)
                nc.scalar.activation(x2t[:, 4 * j:4 * j + 4, :].rearrange("r g c -> r (g c)"), ps[:, M0 + j, :],
                                     ACT.Copy).then_inc(x2t_copied, 1)

            def copy_gram(k, j):
                act.wait_ge(gram_ready, 4 * k + j + 1)
                n = 2 * GRP
                for p in range(2):
                    g = ps[HS * p:HS * p + H, M0 + j % 2, 0:n * GC].rearrange("r (s f) -> r s f", f=GC)
                    for f2 in range(FP):
                        ins = nc.scalar.activation(
                            gram[H * f2:H * f2 + H, 0:NC + 1 - f2, p, n * j:n * j + n].rearrange("r f s -> r s f"),
                            g[:, :, f2:GC:FP], ACT.Copy)
                ins.then_inc(gram_copied, 1)

            def copy_z2(k):
                act.wait_ge(gram_copied, 4 * k + 4)
                nc.scalar.activation(za[0:H, bass.ds(k * P, P)], gram[0:H, NC, :, :].rearrange("o p s -> o (p s)"),
                                     ACT.Copy).then_inc(z2_copied, 1)

            def copy_z3b(k):
                act.wait_ge(z3_ready, k + 1)
                nc.scalar.activation(z3b[:, :], ps[H:P, M0, 0:P], ACT.Copy
                                     ).then_inc(z3b_copied, 1)

            act.wait_ge(consts_loaded, 16)
            act.wait_ge(dense_turned, 1)
            nc.scalar.activation(zb[H:H + DENSE, :], ps[0:DENSE, X1B:X1B + 2, :].rearrange("c b n -> c (b n)"),
                                 ACT.Copy).then_inc(dense_copied, 1)
            split_high(0)
            split_mid(0)
            act.wait_ge(xp_ready, 1)
            nc.scalar.activation(*head_xp(0), ACT.Copy).then_inc(xp_copied, 1)
            act.wait_ge(filled, 1)
            nc.scalar.activation(*head_a0(0), ACT.Copy).then_inc(a0_copied, 1)
            act.wait_ge(summed, 3)
            for twice in range(2):
                ins = nc.scalar.activation(*head_x1(twice, 0), ACT.Copy)
            ins.then_inc(x1_copied, 1)

            def odd_step(u, k, last=False):
                if not last:
                    split_high(k + 1)
                copy_x2(u - 1, 0)
                if not last:
                    split_mid(k + 1)
                    copy_xp(k + 1, 0)
                    copy_a0(u + 1, fills_before(u) + RING["a"], RING["a"])
                build_bd(k)
                if not last:
                    copy_x1(u + 1, 0)

            def even_step(u, k, first=False):
                if not first:
                    copy_x2(u - 1, 1)
                copy_xp(k, 1)
                if not first:
                    copy_x2t(k - 1, 0)
                    copy_x2t(k - 1, 1)
                copy_a0(u + 1, fills_before(u) + RING["a"], RING["a"])
                if not first:
                    for j in range(4):
                        copy_gram(k - 1, j)
                copy_x1(u + 1, 1)
                if not first:
                    copy_z2(k - 1)
                    copy_z3b(k - 1)

            even_step(0, 0, first=True)
            with act.Fori(0, NBLK - 1) as i:
                odd_step(2 * i + 1, i)
                even_step(2 * i + 2, i + 1)
            odd_step(NU - 1, NBLK - 1, last=True)
            copy_x2(NU - 1, 1, last=True)

            def relu_h1(half, m):
                act.wait_ge(h1_ready, half * (TOP1 // P) + m + 1)
                nc.scalar.activation(h1[:, m, half * 512:half * 512 + 512], ps[:, m, :], ACT.Relu, bias=bt1[:, m:m + 1]
                                     ).then_inc(h1_copied, 1)

            def relu_h2(half, m):
                act.wait_ge(h2_ready, half * (TOP2 // P) + m + 1)
                nc.scalar.activation(h2[:, m, half * 512:half * 512 + 512], ps[:, X1B + m, :], ACT.Relu,
                                     bias=bt2[:, m:m + 1]).then_inc(h2_copied, 1)

            act.wait_ge(top_loaded, N_TOP)
            relu_h1(0, 0)
            copy_x2t(NBLK - 1, 0)
            copy_x2t(NBLK - 1, 1)
            relu_h1(0, 1)
            copy_gram(NBLK - 1, 0)
            copy_gram(NBLK - 1, 1)
            relu_h1(0, 2)
            copy_gram(NBLK - 1, 2)
            copy_gram(NBLK - 1, 3)
            relu_h1(0, 3)
            copy_z2(NBLK - 1)
            copy_z3b(NBLK - 1)
            for m in range(TOP2 // P):
                relu_h2(0, m)
            for m in range(TOP1 // P):
                relu_h1(1, m)
            for m in range(TOP2 // P):
                relu_h2(1, m)
            act.wait_ge(y_ready, 1)
            nc.scalar.activation(y[:, :], ps[:, M1, 0:NBLK], ACT.Copy).then_inc(y_copied, 1)

        @block.vector
        def _(dve):
            def split_rest(k):
                dve.wait_ge(high_split, k + 1)
                nc.vector.tensor_tensor(rest[:, :, :].rearrange("s f d -> s d f"),
                                        emb[:, :, :].rearrange("s f d -> s d f"), parts[:, :, 0, :],
                                        ALU.subtract).then_inc(rest_ready, 1)

            def split_low(k):
                dve.wait_ge(mid_split, k + 1)
                nc.vector.tensor_tensor(parts[:, :, 2, :], rest[:, :, :].rearrange("s f d -> s d f"),
                                        parts[:, :, 1, :], ALU.subtract).then_inc(low_split, 1)

            def multiply(what, u, par, n, r, fills, products, shift=0):
                if what in SPREAD:
                    group = [what in g for g in GROUPS].index(True)
                    dve.wait_ge(spread[group], 32 * u + 32)
                    x0 = ab[:, SPREAD.index(what), :].rearrange("r (p n) -> r p n", p=2)
                else:
                    dve.wait_ge(filled, fills + r + 1)
                    x0 = ps[:, slot(r):slot(r) + 2, :]
                if not isinstance(products, int) or products + n >= NZ:
                    dve.wait_ge(summed, products + n - NZ + 1)
                rows = P if what[0] == "c" else ROWS0[int(what[1])]
                other = x1[0:rows, par, :, :] if what[0] == "c" else a0[0:rows, :, :]
                nc.vector.tensor_tensor(prod[0:rows, (n + shift) % NZ, :, :], x0[0:rows], other, ALU.mult
                                        ).then_inc(multiplied, 1)

            def reduce_z1(u, h):
                dve.wait_ge(x1_copied, u + 1)
                nc.vector.tensor_reduce(z1h[:, h, :], ps[:, X1B, :].rearrange("r (s d) -> r s d", d=DH), AX_X, ALU.add
                                        ).then_inc(z1_reduced, 1)

            def add_z1(u, k):
                dve.wait_ge(z1_reduced, u + 1)
                for p in range(2):
                    rows = slice(HS * p, HS * p + H)
                    ins = nc.vector.tensor_tensor(za[H:P, bass.ds(k * P + HS * p, HS)], z1h[rows, 0, :], z1h[rows, 1, :],
                                                  ALU.add)
                ins.then_inc(z1_added, 1)

            def add_z3(k):
                dve.wait_ge(z3b_copied, k + 1)
                nc.vector.tensor_tensor(zb[0:H, bass.ds(k * P, P)], ps[0:H, M0, 0:P], z3b[:, :], ALU.add
                                        ).then_inc(z3_added, 1)

            def step(u, k, par, first=False, last=False):
                order = LAST if last else ORDER
                number, ring = numbers(order), ring_numbers(order)
                for q, what in enumerate(order):
                    if what == "a":
                        continue
                    if what == "c0":
                        dve.wait_ge(x1_copied, u + 1)
                    if what == "b0":
                        dve.wait_ge(a0_copied, u + 2)
                    multiply(what, u, par, number[what], ring.get(what), fills_before(u), products_before(u))
                    if q == 0:
                        reduce_z1(u, par)
                    if q == 0 and par == 1 and not last:
                        split_rest(k + 1)
                    if q == 1 and par == 1 and not last:
                        split_low(k + 1)
                    if q == 3 and par == 1:
                        add_z1(u, k)
                if par == 0 and not first:
                    add_z3(k - 1)

            dve.wait_ge(consts_loaded, 16)
            nc.vector.tensor_copy(sel[:, :], consts[:, 0:MASK]).then_inc(sel_ready, 1)
            nc.vector.tensor_copy(bd[:, :, :, :, F].rearrange("r g p j -> r (g p) j"),
                                  mask.unsqueeze(1).to_broadcast([P, 2 * NG, GRP])).then_inc(bd_ones, 1)
            dve.wait_ge(cin_loaded, N_CIN)
            for c in range(3):
                ins = nc.vector.tensor_tensor(w0[0:BOTH[c], c, :], w0[0:BOTH[c], c, :], w0t[0:BOTH[c], c, :], ALU.add)
            ins.then_inc(w0_ready, 1)
            split_rest(0)
            split_low(0)
            dve.wait_ge(xp_ready, 1)
            nc.vector.tensor_copy(*head_xp(1)).then_inc(shared, 1)
            dve.wait_ge(filled, 1)
            nc.vector.tensor_copy(*head_a0(1)).then_inc(shared, 1)
            dve.wait_ge(a0_copied, 1)
            dve.wait_ge(shared, 2)
            for j in range(3):
                multiply(f"b{j}", 0, 0, j, 1 + j, 0, 0, shift=NZ - 3)
            dve.wait_ge(summed, 3)
            for twice in range(2):
                ins = nc.vector.tensor_copy(*head_x1(twice, 1))
            ins.then_inc(shared, 1)
            dve.wait_ge(shared, 3)
            step(0, 0, 0, first=True)
            with dve.Fori(0, NBLK - 1) as i:
                step(2 * i + 1, i, 1)
                step(2 * i + 2, i + 1, 0)
            step(NU - 1, NBLK - 1, 1, last=True)
            add_z3(NBLK - 1)

        @block.tensor
        def _(pe):
            def fill(what, r, h, free):
                s = slot(r)
                if free is not None:
                    pe.wait_ge(*free)
                if what[0] == "c":
                    col, m = SEL1 + int(what[1:]) * P, P
                else:
                    j = 0 if what == "a" else 1 + int(what[1])
                    col, m = SEL0 + j * R0, R0 if what == "a" else ROWS0[j - 1]
                for p in range(2):
                    ins = nc.tensor.matmul(ps[0:m, s + p, :], sel[0:FR, col:col + m],
                                           xp[:, HS * p:HS * p + HS, DH * h:DH * h + DH],
                                           start=True, stop=True)
                ins.then_inc(filled, 1)

            def contract(what, n):
                j = int(what[1:])
                if what[0] == "c":
                    rows, w, bank, end = P, w1[:, j, :], X2B, NC - 1
                else:
                    rows, w, bank, end = ROWS0[j], w0[0:ROWS0[j], j, :], X1B, 2
                for p in range(2):
                    ins = nc.tensor.matmul(ps[HS * p:HS * p + H, bank, :], w, prod[0:rows, n % NZ, p, :],
                                           start=j == 0, stop=j == end)
                ins.then_inc(summed, 1)

            def build_xp(k, h, head=False):
                for d in range(DH):
                    bank, at = (M0 + 2 * d // DH, P * (d % (DH // 2))) if head else (M1, P * d)
                    ins = nc.tensor.transpose(ps[0:FR, bank, :].bitcast(BF16)[:, at:at + P],
                                              parts[:, DH * h + d, :, :].rearrange("s n f -> s (n f)"),
                                              sel[:, IDENT:IDENT + P])
                ins.then_inc(xp_ready, 1)

            def turn_x0(k):
                for g in range(NG):
                    for p in range(2):
                        c = F * (2 * g + p)
                        s = HS * p + GRP * g
                        ins = nc.tensor.matmul(ps[:, M0, c:c + F], xp[:, s:s + GRP, :].rearrange("r s d -> r (s d)"),
                                               sel[0:FR, SELT:SELT + F], start=True, stop=True)
                ins.then_inc(x0t_ready, 1)

            def turn_x2(k, j):
                for g in range(4):
                    gg = 4 * j + g
                    ins = nc.tensor.transpose(ps[:, M0 + j, P * g:P * g + P],
                                              x2[:, GRP * gg:GRP * gg + GRP, :].rearrange("r s d -> r (s d)"), ident)
                ins.then_inc(x2t_ready, 1)

            def grams(k, j):
                n = GRP * GC
                for g in range(2):
                    gg = 2 * j + g
                    for p in range(2):
                        ins = nc.tensor.matmul(ps[HS * p:HS * p + H, M0 + j % 2, n * g:n * g + n],
                                               x2t[:, gg, HS * p:HS * p + H],
                                               bd[:, gg, p, :, :].rearrange("r j f -> r (j f)"), start=True, stop=True)
                ins.then_inc(gram_ready, 1)

            def layer3(c0, c1):
                half = NC // 2
                for c in range(c0, c1):
                    for n in range(2):
                        ins = nc.tensor.matmul(ps[H * n:H * n + H, M0, 0:P], w2[:, c + half * n, :],
                                               gram[:, c + half * n, :, :].rearrange("r p s -> r (p s)"),
                                               start=c == 0, stop=c == half - 1)
                if c1 == half:
                    ins.then_inc(z3_ready, 1)

            def gram_extra(k, q):
                if q == 3:
                    pe.wait_ge(x2_copied, 2 * k + 2)
                    pe.wait_ge(bd_built, k + 1)
                    turn_x2(k, 0)
                if q == 4:
                    pe.wait_ge(xp_copied, 2 * k + 4)
                    turn_x2(k, 1)
                if q == 5:
                    pe.wait_ge(x2t_copied, 2 * k + 1)
                    grams(k, 0)
                if q == 7:
                    pe.wait_ge(x2t_copied, 2 * k + 2)
                    grams(k, 1)
                if q == 8:
                    pe.wait_ge(gram_copied, 4 * k + 1)
                    grams(k, 2)
                if q == 10:
                    pe.wait_ge(gram_copied, 4 * k + 2)
                    grams(k, 3)
                if q == 13:
                    layer3(0, NC // 4)
                if q == 14:
                    layer3(NC // 4, NC // 2)

            def extra(k, par, q, first, last):
                if par == 0:
                    if not first:
                        gram_extra(k - 1, q)
                else:
                    if q == LAG and not last:
                        pe.wait_ge(low_split, k + 2)
                        build_xp(k + 1, 0)

            def step(u, k, par, first=False, last=False):
                order, before = LAST if last else ORDER, HEAD if first else ORDER
                number, ring = numbers(order), ring_numbers(order)
                back = {w: n - len(numbers(before)) for w, n in numbers(before).items()}
                ring_names = list(ring_numbers(before))[-2:] + list(ring)
                names = before[-LAG:] + order
                for q, what in enumerate(order):
                    if q == 13 and par == 0 and not first:
                        pe.wait_ge(gram_copied, 4 * k)
                    waited = None
                    if what in ring:
                        r = ring[what]
                        reader = ring_names[r]
                        if what == "a":
                            pe.wait_ge(xp_copied, 2 * k + 2 + par)
                        if reader == "a":
                            free = (a0_copied, u + 2)
                        else:
                            waited = back[reader] if r < 2 else number[reader]
                            free = (multiplied, products_before(u) + waited + 1)
                        fill(what, r, 1 - par if what[0] != "c" else par, free)
                    old = names[q]
                    if old != "a":
                        n = back[old] if q < LAG else number[old]
                        if old == "c0" and first:
                            keep_warm(WARM["x1"])
                        if n != waited:
                            pe.wait_ge(multiplied, products_before(u) + n + 1)
                        if old == "c0":
                            pe.wait_ge(xp_copied, 2 * k + 1 + par)
                            if par == 0:
                                build_xp(k, 1)
                            else:
                                turn_x0(k)
                            if not first:
                                pe.wait_ge(x2_copied, u)
                        if old == "b0" and q >= LAG:
                            pe.wait_ge(z1_reduced, u + 1)
                        contract(old, n)
                    extra(k, par, q, first, last)

            def keep_warm(n):
                for _ in range(n):
                    nc.tensor.matmul(ps[:, X2B, :], sel[:, 0:P], sel[:, 0:512], start=True, stop=True)

            pe.wait_ge(consts_loaded, 16)
            pe.wait_ge(dense_loaded, 16)
            for k in range(NBLK):
                ins = nc.tensor.transpose(ps[0:DENSE, X1B + k // 4, P * (k % 4):P * (k % 4) + P], dense[:, k, :], ident)
            ins.then_inc(dense_turned, 1)
            pe.wait_ge(sel_ready, 1)
            pe.wait_ge(dense_copied, 1)
            pe.wait_ge(nearly_gathered, 1)
            keep_warm(WARM["gathers"])
            pe.wait_ge(low_split, 1)
            build_xp(0, 0, head=True)
            pe.wait_ge(w0_ready, 1)
            pe.wait_ge(cin_loaded, N_CIN)
            pe.wait_ge(bd_ones, 1)
            keep_warm(WARM["xp"])
            pe.wait_ge(xp_copied, 1)
            pe.wait_ge(shared, 1)
            fill("a", 0, 0, None)
            fill("b0", 1, 0, None)
            keep_warm(WARM["a0"])
            pe.wait_ge(shared, 2)
            fill("b1", 2, 0, (a0_copied, 1))
            keep_warm(WARM["b0"])
            fill("b2", 3, 0, (multiplied, 1))
            keep_warm(WARM["b1"])
            step(0, 0, 0, first=True)
            with pe.Fori(0, NBLK - 1) as i:
                step(2 * i + 1, i, 1)
                step(2 * i + 2, i + 1, 0)
            step(NU - 1, NBLK - 1, 1, last=True)
            for n in range(NC - LAG, NC):
                pe.wait_ge(multiplied, products_before(NU - 1) + n + 1)
                contract(f"c{n}", n)

            def top1(half, m, parts=(0, 1)):
                cols = slice(m, TOP1, TOP1 // P)
                for part in parts:
                    w, x = ((wt1a, za), (wt1b, zb))[part]
                    ins = nc.tensor.matmul(ps[:, m, :], w[:, cols], x[:, half * 512:half * 512 + 512],
                                           start=part == 0, stop=part == 1)
                if 1 in parts:
                    ins.then_inc(h1_ready, 1)

            def top2(half, m):
                for c in range(TOP1 // P):
                    pe.wait_ge(h1_copied, half * (TOP1 // P) + c + 1)
                    ins = nc.tensor.matmul(ps[:, X1B + m, :], wt2[:, c, m:TOP2:TOP2 // P],
                                           h1[:, c, half * 512:half * 512 + 512],
                                           start=c == 0, stop=c == TOP1 // P - 1)
                ins.then_inc(h2_ready, 1)

            def top3(half):
                for k in range(NBLK // 2 * half, NBLK // 2 * half + NBLK // 2):
                    for c in range(TOP2 // P):
                        ins = nc.tensor.matmul(ps[:, M1, k:k + 1], h2[:, c, P * k:P * k + P], wt3[:, c:c + 1],
                                               start=c == 0, stop=c == TOP2 // P - 1)
                return ins

            last = NBLK - 1
            pe.wait_ge(top_loaded, N_TOP)
            for z in (z1_added, z2_copied, z3_added):
                pe.wait_ge(z, last)
            top1(0, 0)
            pe.wait_ge(x2_copied, 2 * last + 2)
            pe.wait_ge(bd_built, last + 1)
            turn_x2(last, 0)
            turn_x2(last, 1)
            top1(0, 1)
            pe.wait_ge(x2t_copied, 2 * last + 1)
            grams(last, 0)
            pe.wait_ge(x2t_copied, 2 * last + 2)
            grams(last, 1)
            top1(0, 2)
            for j in (2, 3):
                pe.wait_ge(gram_copied, 4 * last + j - 1)
                grams(last, j)
            top1(0, 3)
            pe.wait_ge(gram_copied, 4 * last + 4)
            layer3(0, NC // 2)
            top2(0, 0)
            top2(0, 1)
            pe.wait_ge(z1_added, NBLK)
            pe.wait_ge(z2_copied, NBLK)
            for m in range(TOP1 // P):
                pe.wait_ge(h1_copied, m + 1)
                top1(1, m, parts=(0,))
            pe.wait_ge(z3_added, NBLK)
            for m in range(TOP1 // P):
                top1(1, m, parts=(1,))
            pe.wait_ge(h2_copied, TOP2 // P)
            top3(0)
            for m in range(TOP2 // P):
                top2(1, m)
            pe.wait_ge(h2_copied, 2 * (TOP2 // P))
            top3(1).then_inc(y_ready, 1)


def selections():
    import numpy as np

    c = np.zeros((P, N_CONST), np.float32)
    for part in range(NPART):
        for f in range(F):
            row = F * part + f
            c[row, SEL1 + f * H:SEL1 + f * H + H] = 1
            for j in range(R0 // F):
                c[row, SEL0 + F * j + f] = 1
            for n, shifts in enumerate(SHIFTS):
                for j, shift in enumerate(shifts):
                    c[row, SEL0 + R0 * (1 + n) + F * j + (f - shift) % F] = 1
            c[row, SELT + f] = 1
    c[:, IDENT:IDENT + P] = np.eye(P)
    c[:, MASK:MASK + GRP] = np.repeat(np.eye(GRP), D, axis=0)
    return c


def pair_rows(w):
    import numpy as np

    w = w.reshape(F, F, H)
    f = np.concatenate([np.arange(F) for s in SHIFTS for _ in s])
    g = np.concatenate([(np.arange(F) + shift) % F for s in SHIFTS for shift in s])
    return np.stack([w[f, g], w[g, f]])


_INS = ["dense_ctx", "ids"] + [f"tbl_{i}" for i in range(N_TABLES)] + [
    "W_top1", "b_top1", "W_top2", "b_top2", "W_top3", "L0_rec_W1", "L0_rec_W2"]


def kernel(**inputs):
    import numpy as _np
    import concourse.bacc as _bacc
    from concourse import mybir as _mybir
    from concourse.bass_utils import run_bass_kernel_spmd as _run

    nc = _bacc.Bacc("TRN2", target_bir_lowering=False, num_devices=1)
    arrays = {name: _np.ascontiguousarray(inputs[name]) for name in _INS}
    arrays["W0_pairs"] = _np.ascontiguousarray(pair_rows(_np.asarray(inputs["L0_rec_W0"])))
    arrays["consts"] = selections()
    tensors = {
        name: nc.dram_tensor(f"in_{name}_dram", a.shape, _mybir.dt.from_np(a.dtype), kind="ExternalInput").ap()
        for name, a in arrays.items()
    }
    tensors["x0d"] = nc.dram_tensor("x0d", (2, NC, FP, 2 * NT), _mybir.dt.float32, kind="Internal").ap()
    out = nc.dram_tensor("out_0_dram", (B, 1), _mybir.dt.float32, kind="ExternalOutput").ap()
    cin_tower(nc, tensors, out)
    r = _run(nc, [{f"in_{name}_dram": a for name, a in arrays.items()}], core_ids=[0])
    return r.results[0]["out_0_dram"]
```
